# Optimizing a Trainium2 kernel written in Bass

```python
import numpy as np
import jax
import jax.numpy as jnp

def _softmax(x, axis=-1):
    return jax.nn.softmax(x, axis=axis)

def _gelu(x):
    return jax.nn.gelu(x, approximate=True)

def _silu(x):
    return jax.nn.silu(x)

def _sigmoid(x):
    return jax.nn.sigmoid(x)

def _layernorm(x, axis=-1, eps=1e-05):
    m = jnp.mean(x, axis=axis, keepdims=True)
    v = jnp.var(x, axis=axis, keepdims=True)
    return (x - m) / jnp.sqrt(v + eps)

def _scatter_add(tgt, idx, src, axis=0):
    return tgt.at[idx].add(src)

def _segment_sum(src, seg, n):
    return jax.ops.segment_sum(src, seg, n)
kernel_name = 'mk_xattn_ffn_d1_seqx_r4_6858bc'

def setup_inputs(seed: int=0):
    np.random.seed(seed)
    _w = jnp.asarray

    def _rec_inputs():
        import jax
        import jax.numpy as jnp
        _rk = jax.random.key(seed)
        x = -0.0002928 + 1 * jax.random.normal(jax.random.fold_in(_rk, 1), (8, 256, 256), jnp.float32)
        _lenS = 256 - jax.random.randint(jax.random.fold_in(_rk, 7), (8,), 0, max(1, 256 // 4) + 1, jnp.int32)
        _lenS2 = 120 - jax.random.randint(jax.random.fold_in(_rk, 8), (8,), 0, max(1, 120 // 4) + 1, jnp.int32)
        _ctx_1024P = jax.random.normal(jax.random.fold_in(_rk, 11), (8, 16, 256), jnp.float32)
        _ctx_1024c = jax.random.dirichlet(jax.random.fold_in(_rk, 511), 0.3 * jnp.ones((16,), jnp.float32), (8, 120))
        _ctx_1024t = jnp.einsum('bsk,bkd->bsd', _ctx_1024c, _ctx_1024P)
        _ctx_1024t = _ctx_1024t * jax.lax.rsqrt(jnp.mean(jnp.square(_ctx_1024t)) + 1e-12) * 0.953939
        ctx_1024 = -1.39393e-06 + 0.999914 * (_ctx_1024t + 0.3 * jax.random.normal(jax.random.fold_in(_rk, 611), (8, 120, 256), jnp.float32))
        _validS = jnp.arange(256)[None, :] < _lenS[:, None]
        _validS2 = jnp.arange(120)[None, :] < _lenS2[:, None]
        _causal = jnp.tril(jnp.ones((256, 256), dtype=bool))
        mask_BxSxS2_bk1 = jnp.broadcast_to(_validS2[:, None, :], (8, 256, 120))
        return (x, ctx_1024, mask_BxSxS2_bk1)
    x, ctx_1024, mask_BxSxS2_bk1 = _rec_inputs()

    def _L0_xattn_setup():
        import jax, jax.numpy as jnp
        import numpy as np
        B, T, C = (2, 512, 256)
        H, DQK, DV = (16, 64, 64)

        def _split_heads(x, d):
            b, t, _ = x.shape
            return x.reshape(b, t, H, d).transpose(0, 2, 1, 3)
        key = jax.random.key(seed)
        ks = jax.random.split(key, 8)
        s = 0.03
        Q = jax.random.normal(ks[0], (B, T, C), jnp.float32)
        K = jax.random.normal(ks[1], (B, T, C), jnp.float32)
        V = jax.random.normal(ks[2], (B, T, C), jnp.float32)
        mask = jnp.broadcast_to(jnp.triu(jnp.ones((T, T), bool), 1), (B, T, T))
        Wq = jax.random.normal(ks[3], (C, H * DQK), jnp.float32) * s
        Wk = jax.random.normal(ks[4], (C, H * DQK), jnp.float32) * s
        Wv = jax.random.normal(ks[5], (C, H * DV), jnp.float32) * s
        Wo = jax.random.normal(ks[6], (H * DV, C), jnp.float32) * s
        bq = jnp.zeros((H * DQK,), jnp.float32)
        bk = jnp.zeros((H * DQK,), jnp.float32)
        bv = jnp.zeros((H * DV,), jnp.float32)
        bo = jnp.zeros((C,), jnp.float32)
        return {'Q': Q, 'K': K, 'V': V, 'mask': mask, 'Wq': Wq, 'bq': bq, 'Wk': Wk, 'bk': bk, 'Wv': Wv, 'bv': bv, 'Wo': Wo, 'bo': bo}
    _L0_xattn_all = _L0_xattn_setup()
    _L0_xattn_in = {k: v for k, v in _L0_xattn_all.items() if k in ('Wq', 'bq', 'Wk', 'bk', 'Wv', 'bv', 'Wo', 'bo')}
    del _L0_xattn_all

    def _L0_ffn_setup():
        import jax, jax.numpy as jnp
        import numpy as np
        B, S, H = (2, 512, 256)
        F = 1024
        E = 8
        TOP_K = 2
        SHARED_SCALE = 0.1
        EPS = 1e-09

        def _moe_forward(x3, Wg, W1, b1, W2, b2, Ws1, bs1, Ws2, bs2):
            b, s, h = x3.shape
            x = x3.reshape(-1, h)
            T = x.shape[0]
            logits = x @ Wg
            probs = jax.nn.softmax(logits, axis=-1)
            vals, idx = jax.lax.top_k(probs, TOP_K)
            weights = vals / (jnp.sum(vals, axis=-1, keepdims=True) + EPS)
            cw = jnp.zeros((T, E), dtype=x.dtype).at[jnp.arange(T)[:, None], idx].set(weights)
            hpre = jnp.einsum('th,ehf->tef', x, W1) + b1
            act = jax.nn.silu(hpre)
            y = jnp.einsum('tef,efh->teh', act, W2) + b2
            out = jnp.einsum('te,teh->th', cw, y)
            shared = jax.nn.silu(x @ Ws1 + bs1) @ Ws2 + bs2
            out = out + SHARED_SCALE * shared
            return out.reshape(b, s, h)
        key = jax.random.key(seed)
        ks = jax.random.split(key, 10)
        sc = 0.02
        return {'hidden_states': jax.random.normal(ks[0], (B, S, H), dtype=jnp.float32), 'Wg': jax.random.normal(ks[1], (H, E), dtype=jnp.float32) * sc, 'W1': jax.random.normal(ks[2], (E, H, F), dtype=jnp.float32) * sc, 'b1': jnp.zeros((E, F), dtype=jnp.float32), 'W2': jax.random.normal(ks[3], (E, F, H), dtype=jnp.float32) * sc, 'b2': jnp.zeros((E, H), dtype=jnp.float32), 'Ws1': jax.random.normal(ks[4], (H, F), dtype=jnp.float32) * sc, 'bs1': jnp.zeros((F,), dtype=jnp.float32), 'Ws2': jax.random.normal(ks[5], (F, H), dtype=jnp.float32) * sc, 'bs2': jnp.zeros((H,), dtype=jnp.float32)}
    _L0_ffn_all = _L0_ffn_setup()
    _L0_ffn_in = {k: v for k, v in _L0_ffn_all.items() if k in ('Wg', 'W1', 'b1', 'W2', 'b2', 'Ws1', 'bs1', 'Ws2', 'bs2')}
    del _L0_ffn_all
    return {'x': x, 'ctx_1024': ctx_1024, 'mask_BxSxS2_bk1': mask_BxSxS2_bk1, 'L0_xattn_Wq': _L0_xattn_in['Wq'], 'L0_xattn_bq': _L0_xattn_in['bq'], 'L0_xattn_Wk': _L0_xattn_in['Wk'], 'L0_xattn_bk': _L0_xattn_in['bk'], 'L0_xattn_Wv': _L0_xattn_in['Wv'], 'L0_xattn_bv': _L0_xattn_in['bv'], 'L0_xattn_Wo': _L0_xattn_in['Wo'], 'L0_xattn_bo': _L0_xattn_in['bo'], 'L0_ffn_Wg': _L0_ffn_in['Wg'], 'L0_ffn_W1': _L0_ffn_in['W1'], 'L0_ffn_b1': _L0_ffn_in['b1'], 'L0_ffn_W2': _L0_ffn_in['W2'], 'L0_ffn_b2': _L0_ffn_in['b2'], 'L0_ffn_Ws1': _L0_ffn_in['Ws1'], 'L0_ffn_bs1': _L0_ffn_in['bs1'], 'L0_ffn_Ws2': _L0_ffn_in['Ws2'], 'L0_ffn_bs2': _L0_ffn_in['bs2']}

def reference(x, ctx_1024, mask_BxSxS2_bk1, L0_xattn_Wq, L0_xattn_bq, L0_xattn_Wk, L0_xattn_bk, L0_xattn_Wv, L0_xattn_bv, L0_xattn_Wo, L0_xattn_bo, L0_ffn_Wg, L0_ffn_W1, L0_ffn_b1, L0_ffn_W2, L0_ffn_b2, L0_ffn_Ws1, L0_ffn_bs1, L0_ffn_Ws2, L0_ffn_bs2):
    import jax
    import jax.numpy as jnp

    def _L0_xattn_ref(Q, K, V, mask, Wq, bq, Wk, bk, Wv, bv, Wo, bo):
        import jax, jax.numpy as jnp
        import numpy as np
        B, T, C = (2, 512, 256)
        H, DQK, DV = (16, 64, 64)

        def _split_heads(x, d):
            b, t, _ = x.shape
            return x.reshape(b, t, H, d).transpose(0, 2, 1, 3)
        q = _split_heads(Q @ Wq + bq, DQK)
        k = _split_heads(K @ Wk + bk, DQK)
        v = _split_heads(V @ Wv + bv, DV)
        scores = jnp.einsum('bhqd,bhkd->bhqk', q, k) / jnp.sqrt(jnp.float32(DQK))
        scores = jnp.where(mask[:, None, :, :], -jnp.inf, scores)
        weights = jax.nn.softmax(scores, axis=-1)
        attn = jnp.einsum('bhqk,bhkd->bhqd', weights, v)
        out = attn.transpose(0, 2, 1, 3).reshape(Q.shape[0], Q.shape[1], H * DV)
        return out @ Wo + bo

    def _L0_ffn_ref(hidden_states, Wg, W1, b1, W2, b2, Ws1, bs1, Ws2, bs2):
        import jax, jax.numpy as jnp
        import numpy as np
        B, S, H = (2, 512, 256)
        F = 1024
        E = 8
        TOP_K = 2
        SHARED_SCALE = 0.1
        EPS = 1e-09

        def _moe_forward(x3, Wg, W1, b1, W2, b2, Ws1, bs1, Ws2, bs2):
            b, s, h = x3.shape
            x = x3.reshape(-1, h)
            T = x.shape[0]
            logits = x @ Wg
            probs = jax.nn.softmax(logits, axis=-1)
            vals, idx = jax.lax.top_k(probs, TOP_K)
            weights = vals / (jnp.sum(vals, axis=-1, keepdims=True) + EPS)
            cw = jnp.zeros((T, E), dtype=x.dtype).at[jnp.arange(T)[:, None], idx].set(weights)
            hpre = jnp.einsum('th,ehf->tef', x, W1) + b1
            act = jax.nn.silu(hpre)
            y = jnp.einsum('tef,efh->teh', act, W2) + b2
            out = jnp.einsum('te,teh->th', cw, y)
            shared = jax.nn.silu(x @ Ws1 + bs1) @ Ws2 + bs2
            out = out + SHARED_SCALE * shared
            return out.reshape(b, s, h)
        return _moe_forward(hidden_states, Wg, W1, b1, W2, b2, Ws1, bs1, Ws2, bs2)
    x = x + _L0_xattn_ref(_layernorm(x, axis=-1), ctx_1024, ctx_1024, mask_BxSxS2_bk1, L0_xattn_Wq, L0_xattn_bq, L0_xattn_Wk, L0_xattn_bk, L0_xattn_Wv, L0_xattn_bv, L0_xattn_Wo, L0_xattn_bo)
    x = x + _L0_ffn_ref(_layernorm(x, axis=-1), L0_ffn_Wg, L0_ffn_W1, L0_ffn_b1, L0_ffn_W2, L0_ffn_b2, L0_ffn_Ws1, L0_ffn_bs1, L0_ffn_Ws2, L0_ffn_bs2)
    return x

_drawn_inputs = setup_inputs


def setup_inputs(seed=0):
    import zlib

    import numpy as np

    out = dict(_drawn_inputs(seed))
    spreads = {'L0_xattn_bq': (0.0, 0.61),
     'L0_xattn_bk': (0.0, 0.8),
     'L0_xattn_bv': (0.0, 0.1),
     'L0_xattn_bo': (0.0, 0.1),
     'L0_ffn_b1': (0.0, 0.334),
     'L0_ffn_b2': (0.0, 0.1),
     'L0_ffn_bs1': (0.0, 0.8),
     'L0_ffn_bs2': (0.0, 0.8)}
    factors = {'L0_ffn_Ws1': 5.721, 'L0_ffn_Ws2': 5.41}
    for name, (base, spread) in spreads.items():
        noise = np.random.default_rng([zlib.crc32(name.encode()), seed]).standard_normal(out[name].shape)
        drawn = base * np.exp(spread * noise) if base else spread * noise
        out[name] = jnp.asarray(drawn.astype(out[name].dtype))
    for name, factor in factors.items():
        out[name] = (out[name] * factor).astype(out[name].dtype)
    return out
```

```python
import concourse.bass as bass
from concourse import mybir
from contextlib import ExitStack

F32 = mybir.dt.float32
F32R = mybir.dt.float32r
BF16 = mybir.dt.bfloat16
I32 = mybir.dt.int32
U32 = mybir.dt.uint32
U8 = mybir.dt.uint8
ALU = mybir.AluOpType
ACT = mybir.ActivationFunctionType
AX = mybir.AxisListType


def xattn_moe_kernel(nc, x, ctx_in, mask, wq, bq, wk, bk, wv, bv, wo, bo,
                     wg, w1, b1, w2, b2, ws1, bs1, ws2, bs2, out):
    B, S, C = x.shape
    SK = ctx_in.shape[1]
    HD = wq.shape[1]
    D = 64
    P = 128
    KC = C // P
    PAIRS = HD // P
    TILES = B * S // P
    GB = 2
    G = B // GB
    GT = TILES // G
    QT = S // P
    GW = GT * P
    SK2 = 2 * SK
    VW = 3 * D
    EPS = 1e-5
    SHARED = 0.1
    NE = wg.shape[1]
    F = w1.shape[2]
    NBLK = 2 * TILES + NE - 1
    NOBODY = B * S
    ROW = C + 9
    MASKED = -1e30

    es = ExitStack()
    with es:
        def sem(name):
            return es.enter_context(nc.semaphore(name))

        def sb(name, shape, dt, stack=es):
            return stack.enter_context(nc.sbuf_tensor(name, shape, dt))

        ident = sb("ident", [P, P], F32)
        identb = sb("identb", [P, P], BF16)
        xall = sb("xall", [P, TILES, C], F32)
        xrows = sb("xrows", [P, TILES, ROW], F32)
        wt_hi = sb("wt_hi", [P, 4, KC * HD], F32R)
        wt_lo = sb("wt_lo", [P, 4, KC * HD], F32R)
        stage = sb("stage", [P, 2, KC * HD], F32)

        startsi = sb("startsi", [P, NE], I32)
        ebi = sb("ebi", [P, 2, NBLK], I32)
        slots = nc.dram_tensor("slots", (NBLK * P, ROW), F32, kind="Internal").ap()

        a = ExitStack()
        xhat = sb("xhat", [P, GT, C], F32, a)
        ctxb = sb("ctxb", [SK, GB, C], F32, a)
        masku = sb("masku", [P, GT, SK], U8, a)
        maskb = sb("maskb", [P, GT, 2, SK], BF16, a)
        xT_hi = sb("xT_hi", [P, KC, GW], F32R, a)
        xT_lo = sb("xT_lo", [P, KC, GW], F32R, a)
        cT_hi = sb("cT_hi", [P, KC, GB * SK], F32R, a)
        cT_lo = sb("cT_lo", [P, KC, GB * SK], F32R, a)
        v_hi = sb("v_hi", [SK, GB, PAIRS, VW], F32R, a)
        v_lo = sb("v_lo", [SK, GB, PAIRS, VW], F32R, a)
        q_hi = sb("q_hi", [P, GW], F32R, a)
        q_lo = sb("q_lo", [P, GW], F32R, a)
        k_hi = sb("k_hi", [P, GB, SK2], F32R, a)
        k_lo = sb("k_lo", [P, GB, SK2], F32R, a)
        pT_hi = sb("pT_hi", [SK, GB, 2, QT, P], F32R, a)
        pT_lo = sb("pT_lo", [SK, GB, 2, QT, P], F32R, a)
        aT_hi = sb("aT_hi", [P, PAIRS, GW], F32R, a)
        aT_lo = sb("aT_lo", [P, PAIRS, GW], F32R, a)
        bqk = sb("bqk", [P, 3, PAIRS], F32, a)
        bo_bc = sb("bo_bc", [P, C], F32, a)
        stats = sb("stats", [P, GT, 6], F32, a)
        mv = sb("mv", [P, GT, 2], F32, a)
        rstd = sb("rstd", [P, GT], F32, a)
        fence = sb("fence", [P, 1], F32, a)
        vareps = sb("vareps", [P, GT], F32, a)
        mhalf = sb("mhalf", [P, GT], F32, a)
        epst = sb("epst", [P, GT], F32, a)
        smax = sb("smax", [P, 2, GT, 2], F32, a)
        ssum = sb("ssum", [P, 2, GT, 2], F32, a)
        rsum = sb("rsum", [P, 2, GT, 2], F32, a)
        a.close()

        flat = stage[:, :, :].rearrange("p a n -> p (a n)")
        x2g = flat[:, 2 * GT * SK2:2 * GT * SK2 + GT * C].rearrange("p (t c) -> p t c", t=GT)
        pad_at = 2 * GT * SK2 + GT * C
        padrow = flat[:, pad_at:pad_at + ROW]
        pr = flat[:, 0:2 * GT * SK2] \
            .rearrange("p (r t h k) -> p r t h k", r=2, t=GT, h=2)

        ps = ExitStack()

        def pb(name):
            return ps.enter_context(nc.psum_tensor(name, [P, 512], F32))
        bank_q, bank_k, bank_m, bank_o = pb("bank_q"), pb("bank_k"), pb("bank_m"), pb("bank_o")
        bank_s = [pb("bank_s0"), pb("bank_s1")]
        bank_t = [pb("bank_t0"), pb("bank_t1")]
        ps.close()

        names = """pad padded ve x2_kept bias_in mask_in ctx_in w_hi w_lo const zeros ln1 xbo xcopied xt ct
                   xt_hi xt_lo ct_hi ct_lo vp v_hi_s v_lo_s mb qk_q qk_k q_hi_s k_hi_s q_lo_s k_lo_s
                   sc mx sub ex sm rc nrm tp p_hi p_lo pv a_hi a_lo wo_d x2 ln2 dv_st dv_ag dv_rs""".split()
        s = {n: sem(n) for n in names}
        x_in = [sem(f"x_in{g}") for g in range(G)]
        wraw_in = [sem(f"wraw_in{i}") for i in range(4)]

        x_v = x.rearrange("b (t p) c -> p (b t) c", p=P)
        m_v = mask.rearrange("b (t p) k -> p (b t) k", p=P)
        w_views = [wv.rearrange("(k p) n -> p k n", p=P), wk.rearrange("(k p) n -> p k n", p=P),
                   wq.rearrange("(k p) n -> p k n", p=P), wo.rearrange("(k p) n -> p k n", p=P)]
        ctx_v = ctx_in.rearrange("b k c -> k b c")

        def w_of(i, lo, view=None):
            return (wt_lo if lo else wt_hi)[:, i, :].rearrange("p (k n) -> p k n", n=(w_views[i] if view is None else view).shape[2])

        def count_from_one(eng, names):
            for n in names.split():
                eng.sem_inc(s[n], 1)

        def three(pe, o, st, mo, first, last):
            nc.tensor.matmul(o, st(0), mo(0), start=first, stop=False)
            nc.tensor.matmul(o, st(0), mo(1), start=False, stop=False)
            return nc.tensor.matmul(o, st(1), mo(0), start=False, stop=last)

        with nc.Block() as block:
            @block.sync
            def _(sp):
                sp.dma_start(stage[:, 0, :].rearrange("p (k n) -> p k n", k=KC), w_views[0]).then_inc(wraw_in[0], 16)
                for t in range(0, TILES, GT):
                    sp.dma_start(xall[:, t:t + GT, :], x_v[:, t:t + GT, :]).then_inc(x_in[t // GT], 16)
                    if t == 0:
                        sp.dma_start(ctxb[:, :, :], ctx_v[:, 0:GB, :]).then_inc(s["ctx_in"], 16)
                        sp.dma_start(stage[:, 1, :].rearrange("p (k n) -> p k n", k=KC), w_views[1]).then_inc(wraw_in[1], 16)
                        for i, bb in enumerate((bq, bk, bv)):
                            sp.dma_start(bqk[:, i, :], bb.rearrange("(a p) -> p a", p=P), allow_slow_non_contiguous=True).then_inc(s["bias_in"], 16)
                        sp.dma_start(masku[:, :, :], m_v[:, 0:GT, :]).then_inc(s["mask_in"], 16)
                        sp.dma_start(bo_bc[:, :], bo.rearrange("(a n) -> a n", a=1).broadcast_to([P, C])).then_inc(s["bias_in"], 16)
                for i in (2, 3):
                    sp.wait_ge(s["w_hi"], i - 1)
                    sp.wait_ge(s["w_lo"], i - 1)
                    k = w_views[i].shape[1]
                    sp.dma_start(stage[:, i % 2, :].rearrange("p (k n) -> p k n", k=k), w_views[i]).then_inc(wraw_in[i], 16)
                sp.wait_ge(s["pad"], 2)
                sp.dma_start(slots.rearrange("(b p) n -> p b n", p=P), padrow[:, :].rearrange("p (a n) -> p a n", a=1)
                             .broadcast_to([P, NBLK, ROW])).then_inc(s["padded"], 16)
                with sp.Fori(1, G) as g:
                    sp.wait_ge(s["ct"], g)
                    sp.dma_start(ctxb[:, :, :], ctx_v[:, bass.ds(g * GB, GB), :]).then_inc(s["ctx_in"], 16)
                    sp.wait_ge(s["mb"], g)
                    sp.dma_start(masku[:, :, :], m_v[:, bass.ds(g * GT, GT), :]).then_inc(s["mask_in"], 16)

                sp.wait_ge(s["padded"], 16)

            @block.gpsimd
            def _(pool):
                count_from_one(pool, "x2_kept")
                def rsqrt(stat):
                    pool.wait_ge(s["dv_ag"], stat * GT + GT)
                    nc.gpsimd.tensor_tensor(vareps[:, :], mv[:, :, 1], epst[:, :], ALU.add).then_inc(s["ve"], 1)
                    pool.wait_ge(s["ve"], stat + 1)
                    nc.gpsimd.tensor_tensor(rstd[:, :], vareps[:, :], mhalf[:, :], ALU.pow).then_inc(s["dv_rs"], 1)

                nc.gpsimd.memset(mhalf[:, :], -0.5).then_inc(s["zeros"], 1)
                nc.gpsimd.memset(epst[:, :], EPS).then_inc(s["zeros"], 1)
                nc.gpsimd.memset(ident[:, :], 0.0).then_inc(s["zeros"], 1)
                nc.gpsimd.memset(identb[:, :], 0.0).then_inc(s["zeros"], 1)
                pool.wait_ge(s["zeros"], 4)
                for m in (ident, identb):
                    nc.gpsimd.affine_select(out=m[:, :], in_=m[:, :], compare_op=ALU.not_equal, fill=1.0, base=0,
                                            pattern=[[-1, P]], channel_multiplier=1).then_inc(s["const"], 1)
                for z in (k_hi, k_lo, v_hi, v_lo):
                    nc.gpsimd.memset(z[:].bitcast(F32), 0.0).then_inc(s["const"], 1)
                for g in range(G):
                    rsqrt(g)
                for i in range(4):
                    pool.wait_ge(s["w_hi"], i + 1)
                    nc.gpsimd.tensor_tensor(wt_lo[:, i, :], stage[:, i % 2, :], wt_hi[:, i, :].bitcast(F32),
                                            ALU.subtract).then_inc(s["w_lo"], 1)
                    if i == 0:
                        pool.wait_ge(s["bias_in"], 64)
                pool.wait_ge(s["w_lo"], 4)
                nc.gpsimd.memset(padrow[:, :], 0.0).then_inc(s["pad"], 1)
                pool.wait_ge(s["pad"], 1)
                nc.gpsimd.memset(padrow[:, C:C + 1].bitcast(I32), NOBODY).then_inc(s["pad"], 1)
                for t in range(G):
                    pool.wait_ge(s["ln1"], t + 1)
                    nc.gpsimd.tensor_tensor(xall[:, t * GT:(t + 1) * GT, :], xall[:, t * GT:(t + 1) * GT, :],
                                            bo_bc[:, :].rearrange("p (a c) -> p a c", a=1).broadcast_to([P, GT, C]),
                                            ALU.add).then_inc(s["xbo"], 1)
                with pool.Fori(0, G) as g:
                    pool.wait_ge(s["xt"], 1 + g * KC)
                    nc.gpsimd.tensor_copy(xhat[:, :, :], xrows[:, bass.ds(g * GT, GT), 0:C]).then_inc(s["xcopied"], 1)
                    for p in range(PAIRS):
                        for b in range(GB):
                            pool.wait_ge(s["rc"], (g * PAIRS + p) * GB + b + 1)
                            pt = pr[:, p % 2, b * QT:(b + 1) * QT, :, :]
                            nc.gpsimd.tensor_tensor(
                                pt, pt, rsum[:, p % 2, b * QT:(b + 1) * QT, :].rearrange("p t (h a) -> p t h a", a=1)
                                .broadcast_to([P, QT, 2, SK]), ALU.mult).then_inc(s["nrm"], 1)
                    pool.wait_ge(s["x2"], 1 + g * 2 + 2)
                    nc.gpsimd.tensor_copy(xall[:, bass.ds(g * GT, GT), :], x2g).then_inc(s["x2_kept"], 1)
                    rsqrt(g + G)

            @block.scalar
            def _(act):
                def split_weight(i):
                    act.wait_ge(wraw_in[i], 16)
                    nc.scalar.activation(wt_hi[:, i, :], stage[:, i % 2, :], ACT.Copy).then_inc(s["w_hi"], 1)
                for i in range(4):
                    split_weight(i)
                act.wait_ge(s["bias_in"], 64)
                act.wait_ge(s["const"], 6)
                with act.Fori(0, G) as g:
                    for k in range(KC):
                        act.wait_ge(s["xt"], 1 + g * KC + k + 1)
                        nc.scalar.activation(xT_hi[:, k, :], bank_s[k][:, :], ACT.Copy).then_inc(s["xt_hi"], 1)
                    act.wait_ge(s["ct"], g + 1)
                    nc.scalar.activation(cT_hi[:, :, :], bank_m[:, 0:KC * GB * SK], ACT.Copy).then_inc(s["ct_hi"], 1)
                    for j in range(2 * GB):
                        act.wait_ge(s["vp"], g * 2 * GB + j + 1)
                        b, h = j // 2, j % 2
                        bank = (bank_t[0], bank_t[1], bank_m, bank_o)[j]
                        vin = bank[0:SK, :].rearrange("p (a e d) -> p a e d", e=2, d=D)
                        vout = v_hi[:, b, h * PAIRS // 2:(h + 1) * PAIRS // 2, :] \
                            .rearrange("p a (e d) -> p a e d", d=D)[:, :, 0:3:2, :]
                        nc.scalar.activation(vout, vin, ACT.Copy).then_inc(s["v_hi_s"], 1)

                    def qk_hi(p):
                        act.wait_ge(s["qk_q"], g * PAIRS + p + 1)
                        act.wait_ge(s["sc"], 1 + (g * PAIRS + p) * GB)
                        nc.scalar.activation(q_hi[:, :], bank_q[:, :], ACT.Identity, bias=bqk[:, 0, p:p + 1]).then_inc(s["q_hi_s"], 1)
                        act.wait_ge(s["qk_k"], g * PAIRS + p + 1)
                        for e in range(2):
                            r = slice(e * D, (e + 1) * D)
                            nc.scalar.activation(k_hi[r, :, e * SK:(e + 1) * SK],
                                                 bank_k[r, 0:GB * SK].rearrange("p (b k) -> p b k", b=GB),
                                                 ACT.Identity, bias=bqk[r, 1, p:p + 1]).then_inc(s["k_hi_s"], 1)

                    def exps(p):
                        for b in range(GB):
                            act.wait_ge(s["sub"], 1 + (g * PAIRS + p) * GB + b + 1)
                            pt = pr[:, p % 2, b * QT:(b + 1) * QT, :, :]
                            nc.scalar.activation(pt, pt, ACT.Exp, scale=D ** -0.5).then_inc(s["ex"], 1)

                    def pt_hi(p):
                        for b in range(GB):
                            act.wait_ge(s["tp"], 1 + (g * PAIRS + p) * GB + b + 1)
                            act.wait_ge(s["pv"], 1 + g * PAIRS + p)
                            nc.scalar.activation(pT_hi[:, b, :, :, :], bank_t[b][0:SK, :], ACT.Copy).then_inc(s["p_hi"], 1)

                    def a_hi(p):
                        act.wait_ge(s["pv"], 1 + g * PAIRS + p + 1)
                        if p == 0:
                            act.wait_ge(s["wo_d"], 1 + g * 2)
                        nc.scalar.activation(aT_hi[:, p, :], bank_o[:, :], ACT.Identity, bias=bqk[:, 2, p:p + 1]).then_inc(s["a_hi"], 1)

                    qk_hi(0)
                    for p in range(PAIRS):
                        exps(p)
                        if p:
                            pt_hi(p - 1)
                        if p + 1 < PAIRS:
                            qk_hi(p + 1)
                        if p:
                            a_hi(p - 1)
                    pt_hi(PAIRS - 1)
                    a_hi(PAIRS - 1)

            @block.vector
            def _(dve):
                count_from_one(dve, "sub x2 p_lo a_lo q_lo_s k_lo_s")
                def norm(tile, done, stat, dst):
                    for t in range(GT):
                        nc.vector.bn_stats(stats[:, t, :], tile(t)).then_inc(s["dv_st"], 1)
                    dve.wait_ge(s["dv_st"], stat * GT + GT)
                    nc.vector.memset(fence[:, :], 0.0)
                    for t in range(GT):
                        nc.vector.bn_aggr(mv[:, t, :], stats[:, t, :]).then_inc(s["dv_ag"], 1)
                    dve.wait_ge(s["dv_rs"], stat + 1)
                    for t in range(GT):
                        last = nc.vector.tensor_scalar(dst(t), tile(t), mv[:, t, 0:1], rstd[:, t:t + 1],
                                                       ALU.subtract, ALU.mult)
                    last.then_inc(s[done], 1)

                for g in range(G):
                    dve.wait_ge(x_in[g], 16)
                    norm(lambda t: xall[:, g * GT + t, :], "ln1", g, lambda t: xrows[:, g * GT + t, 0:C])
                dve.wait_ge(s["bias_in"], 64)
                dve.wait_ge(s["const"], 6)
                with dve.Fori(0, G) as g:
                    dve.wait_ge(s["sc"], 1 + g * PAIRS * GB)
                    dve.wait_ge(s["mask_in"], 16 * (g + 1))
                    nc.vector.tensor_scalar(maskb[:, :, :, :], masku[:, :, :]
                                            .rearrange("p t (a k) -> p t a k", a=1).broadcast_to([P, GT, 2, SK]),
                                            MASKED, None, ALU.mult).then_inc(s["mb"], 1)
                    for k in range(KC):
                        dve.wait_ge(s["xt_hi"], g * KC + k + 1)
                        nc.vector.tensor_tensor(xT_lo[:, k, :], bank_s[k][:, :], xT_hi[:, k, :].bitcast(F32),
                                                ALU.subtract).then_inc(s["xt_lo"], 1)
                    dve.wait_ge(s["ct_hi"], g + 1)
                    nc.vector.tensor_tensor(cT_lo[:, :, :].rearrange("p k n -> p (k n)"), bank_m[:, 0:KC * GB * SK],
                                            cT_hi[:, :, :].bitcast(F32).rearrange("p k n -> p (k n)"),
                                            ALU.subtract).then_inc(s["ct_lo"], 1)
                    for j in range(2 * GB):
                        dve.wait_ge(s["v_hi_s"], g * 2 * GB + j + 1)
                        b, h = j // 2, j % 2
                        bank = (bank_t[0], bank_t[1], bank_m, bank_o)[j]
                        vin = bank[0:SK, :].rearrange("p (a e d) -> p a e d", e=2, d=D)
                        sel = lambda v: v[:, b, h * PAIRS // 2:(h + 1) * PAIRS // 2, :] \
                            .rearrange("p a (e d) -> p a e d", d=D)[:, :, 0:3:2, :]
                        nc.vector.tensor_tensor(sel(v_lo), vin, sel(v_hi).bitcast(F32), ALU.subtract).then_inc(s["v_lo_s"], 1)

                    def qk_lo(p):
                        dve.wait_ge(s["q_hi_s"], g * PAIRS + p + 1)
                        nc.vector.scalar_tensor_tensor(out=q_lo[:, :], in0=bank_q[:, :], scalar=bqk[:, 0, p:p + 1],
                                                       in1=q_hi[:, :].bitcast(F32), op0=ALU.add, op1=ALU.subtract).then_inc(s["q_lo_s"], 1)
                        dve.wait_ge(s["k_hi_s"], 2 * (g * PAIRS + p + 1))
                        for e in range(2):
                            r = slice(e * D, (e + 1) * D)
                            nc.vector.scalar_tensor_tensor(
                                out=k_lo[r, :, e * SK:(e + 1) * SK],
                                in0=bank_k[r, 0:GB * SK].rearrange("p (b k) -> p b k", b=GB), scalar=bqk[r, 1, p:p + 1],
                                in1=k_hi[r, :, e * SK:(e + 1) * SK].bitcast(F32), op0=ALU.add, op1=ALU.subtract).then_inc(s["k_lo_s"], 1)

                    def max_sub(p):
                        n = g * PAIRS + p
                        dve.wait_ge(s["tp"], 1 + ((n - 1) * GB if p else n * GB))
                        if p == 0:
                            dve.wait_ge(s["w_lo"], 4)
                        for b in range(GB):
                            dve.wait_ge(s["sc"], 1 + n * GB + b + 1)
                            sc = bank_s[b][:, 0:QT * SK2].rearrange("p (t h k) -> p t h k", t=QT, h=2)
                            m = smax[:, p % 2, b * QT:(b + 1) * QT, :]
                            nc.vector.tensor_reduce(m, sc, AX.X, ALU.max).then_inc(s["mx"], 1)
                            dve.wait_ge(s["mx"], n * GB + b + 1)
                            nc.vector.tensor_tensor(pr[:, p % 2, b * QT:(b + 1) * QT, :, :], sc,
                                                    m.rearrange("p t (h a) -> p t h a", a=1).broadcast_to([P, QT, 2, SK]),
                                                    ALU.subtract).then_inc(s["sub"], 1)

                    def sums(p):
                        n = g * PAIRS + p
                        for b in range(GB):
                            dve.wait_ge(s["ex"], n * GB + b + 1)
                            nc.vector.tensor_reduce(ssum[:, p % 2, b * QT:(b + 1) * QT, :],
                                                    pr[:, p % 2, b * QT:(b + 1) * QT, :, :], AX.X, ALU.add).then_inc(s["sm"], 1)
                            dve.wait_ge(s["sm"], n * GB + b + 1)
                            nc.vector.reciprocal(rsum[:, p % 2, b * QT:(b + 1) * QT, :],
                                                 ssum[:, p % 2, b * QT:(b + 1) * QT, :]).then_inc(s["rc"], 1)

                    def pt_lo(p):
                        for b in range(GB):
                            dve.wait_ge(s["p_hi"], (g * PAIRS + p) * GB + b + 1)
                            nc.vector.tensor_tensor(pT_lo[:, b, :, :, :].rearrange("p h t q -> p (h t q)"), bank_t[b][0:SK, :],
                                                    pT_hi[:, b, :, :, :].bitcast(F32).rearrange("p h t q -> p (h t q)"),
                                                    ALU.subtract).then_inc(s["p_lo"], 1)

                    def a_lo(p):
                        dve.wait_ge(s["a_hi"], g * PAIRS + p + 1)
                        nc.vector.scalar_tensor_tensor(out=aT_lo[:, p, :], in0=bank_o[:, :], scalar=bqk[:, 2, p:p + 1],
                                                       in1=aT_hi[:, p, :].bitcast(F32), op0=ALU.add, op1=ALU.subtract).then_inc(s["a_lo"], 1)

                    qk_lo(0)
                    for p in range(PAIRS):
                        max_sub(p)
                        if p:
                            pt_lo(p - 1)
                        if p + 1 < PAIRS:
                            qk_lo(p + 1)
                        sums(p)
                        if p:
                            a_lo(p - 1)
                    pt_lo(PAIRS - 1)
                    a_lo(PAIRS - 1)
                    for h in range(2):
                        dve.wait_ge(s["wo_d"], 1 + g * 2 + h + 1)
                        if h == 0:
                            dve.wait_ge(s["xbo"], G)
                            dve.wait_ge(s["x2_kept"], 1 + g)
                            dve.wait_ge(s["xcopied"], g + 1)
                        xa = xall[:, bass.ds(g * GT + 2 * h, 2), :]
                        nc.vector.tensor_tensor(x2g[:, 2 * h:2 * h + 2, :],
                                                (bank_m, bank_k)[h][:, :].rearrange("p (t c) -> p t c", t=2), xa,
                                                ALU.add).then_inc(s["x2"], 1)
                    dve.wait_ge(s["x2"], 1 + g * 2 + 2)
                    norm(lambda t: x2g[:, t, :], "ln2", g + G,
                         lambda t: xrows[:, bass.ds(g * GT + t, 1), 0:C].rearrange("p a c -> p (a c)"))

            @block.tensor
            def _(pe):
                count_from_one(pe, "xt sc pv wo_d tp")
                pe.wait_ge(s["const"], 6)
                with pe.Fori(0, G) as g:
                    pe.wait_ge(s["xcopied"], g + 1)
                    pe.wait_ge(s["sub"], 1 + g * PAIRS * GB)
                    for k in range(KC):
                        for t in range(GT):
                            last = nc.tensor.transpose(bank_s[k][:, t * P:(t + 1) * P], xhat[:, t, k * P:(k + 1) * P], ident[:, :])
                        last.then_inc(s["xt"], 1)
                    pe.wait_ge(s["ctx_in"], 16 * (g + 1))
                    pe.wait_ge(s["x2"], 1 + g * 2)
                    for k in range(KC):
                        for b in range(GB):
                            o = (k * GB + b) * SK
                            last = nc.tensor.transpose(bank_m[:, o:o + SK], ctxb[:, b, k * P:(k + 1) * P], ident[0:SK, 0:SK])
                    last.then_inc(s["ct"], 1)

                    pe.wait_ge(s["ct_lo"], g + 1)
                    pe.wait_ge(s["w_lo"], 1)
                    pe.wait_ge(s["p_lo"], 1 + g * PAIRS * GB)
                    pe.wait_ge(s["a_lo"], 1 + g * PAIRS)
                    for j in range(2 * GB):
                        b, h = j // 2, j % 2
                        bank = (bank_t[0], bank_t[1], bank_m, bank_o)[j]
                        for k in range(KC):
                            last = three(pe, bank[0:SK, :],
                                         lambda lo: (cT_lo if lo else cT_hi)[:, k, b * SK:(b + 1) * SK],
                                         lambda lo: w_of(0, lo)[:, k, h * 512:(h + 1) * 512], k == 0, k == KC - 1)
                        last.then_inc(s["vp"], 1)

                    def qk(p):
                        n = g * PAIRS + p
                        pe.wait_ge(s["q_lo_s"], 1 + n)
                        if p == 0:
                            pe.wait_ge(s["xt_lo"], (g + 1) * KC)
                            pe.wait_ge(s["w_lo"], 3)
                        for k in range(KC):
                            last = three(pe, bank_q[:, :], lambda lo: w_of(2, lo)[:, k, p * P:(p + 1) * P],
                                         lambda lo: (xT_lo if lo else xT_hi)[:, k, :], k == 0, k == KC - 1)
                        last.then_inc(s["qk_q"], 1)
                        pe.wait_ge(s["k_lo_s"], 1 + 2 * n)
                        for k in range(KC):
                            last = three(pe, bank_k[:, 0:GB * SK], lambda lo: w_of(1, lo)[:, k, p * P:(p + 1) * P],
                                         lambda lo: (cT_lo if lo else cT_hi)[:, k, :], k == 0, k == KC - 1)
                        last.then_inc(s["qk_k"], 1)

                    def scores(p):
                        n = g * PAIRS + p
                        pe.wait_ge(s["q_lo_s"], 1 + n + 1)
                        pe.wait_ge(s["k_lo_s"], 1 + 2 * (n + 1))
                        if p == 0:
                            pe.wait_ge(s["mb"], g + 1)
                        for b in range(GB):
                            pe.wait_ge(s["sub"], 1 + ((n - 1) * GB + b + 1 if p else n * GB))
                            for t in range(QT):
                                o = bank_s[b][:, t * SK2:(t + 1) * SK2]
                                q = slice((b * QT + t) * P, (b * QT + t + 1) * P)
                                three(pe, o, lambda lo: (q_lo if lo else q_hi)[:, q],
                                      lambda lo: (k_lo if lo else k_hi)[:, b, :], True, False)
                                last = nc.tensor.matmul(o, identb[:, :], maskb[:, b * QT + t, :, :], start=False, stop=True)
                            last.then_inc(s["sc"], 1)

                    def transposes(p):
                        n = g * PAIRS + p
                        for b in range(GB):
                            pe.wait_ge(s["nrm"], n * GB + b + 1)
                            if p:
                                pe.wait_ge(s["p_lo"], 1 + (n - 1) * GB + b + 1)
                            else:
                                pe.wait_ge(s["v_lo_s"], g * 2 * GB + 2)
                            for h in range(2):
                                for t in range(QT):
                                    o = (h * QT + t) * P
                                    last = nc.tensor.transpose(bank_t[b][0:SK, o:o + P], pr[:, p % 2, b * QT + t, h, :], ident[:, :])
                            last.then_inc(s["tp"], 1)

                    def values(p):
                        n = g * PAIRS + p
                        pe.wait_ge(s["a_lo"], 1 + n)
                        if p == 0:
                            pe.wait_ge(s["v_lo_s"], (g + 1) * 2 * GB)
                        for b in range(GB):
                            pe.wait_ge(s["p_lo"], 1 + n * GB + b + 1)
                            o = bank_o[:, b * S:(b + 1) * S]
                            for h in range(2):
                                last = three(pe, o, lambda lo: (v_lo if lo else v_hi)[:, b, p, h * D:h * D + P],
                                             lambda lo: (pT_lo if lo else pT_hi)[:, b, h, :, :], h == 0, h == 1)
                        last.then_inc(s["pv"], 1)

                    qk(0)
                    for p in range(PAIRS):
                        scores(p)
                        if p:
                            transposes(p - 1)
                        if p + 1 < PAIRS:
                            qk(p + 1)
                        if p:
                            values(p - 1)
                    transposes(PAIRS - 1)
                    values(PAIRS - 1)
                    pe.wait_ge(s["a_lo"], 1 + (g + 1) * PAIRS)
                    pe.wait_ge(s["v_lo_s"], (g + 1) * 2 * GB)
                    pe.wait_ge(s["w_lo"], 4)
                    pe.wait_ge(s["k_lo_s"], 1 + 2 * (g + 1) * PAIRS)
                    for h in range(2):
                        bank = (bank_m, bank_k)[h]
                        for t in range(2):
                            for p in range(PAIRS):
                                q = slice((2 * h + t) * P, (2 * h + t + 1) * P)
                                last = three(pe, bank[:, t * C:(t + 1) * C], lambda lo: (aT_lo if lo else aT_hi)[:, p, q],
                                             lambda lo: w_of(3, lo)[:, p, :], p == 0, p == PAIRS - 1)
                        last.then_inc(s["wo_d"], 1)

        NF = F // P
        TE = TILES * NE
        out_f = out.rearrange("b s c -> (b s) c")
        out_v = out.rearrange("b (t p) c -> p (b t) c", p=P)
        r = ExitStack()
        zT_hi = sb("zT_hi", [P, KC, TILES * P], F32R, r)
        zT_lo = sb("zT_lo", [P, KC, TILES * P], F32R, r)
        sh = sb("sh", [P, 2, GW], F32, r)
        hT_hi = sb("hT_hi", [P, NF, GW], F32R, r)
        hT_lo = sb("hT_lo", [P, NF, GW], F32R, r)
        wg_raw = sb("wg_raw", [P, KC, NE], F32, r)
        wg_hi = sb("wg_hi", [P, KC, NE], F32R, r)
        wg_lo = sb("wg_lo", [P, KC, NE], F32R, r)
        bs1c = sb("bs1c", [P, NF], F32, r)
        bs2_bc = sb("bs2_bc", [P, C], F32, r)
        rt = {n: sb("rt_" + n, [P, TILES, NE], F32, r) for n in ("d", "p", "eq", "oh1", "oh2", "p2", "tmp")}
        rm = {n: sb("rm_" + n, [P, TILES], F32, r) for n in ("m", "sum", "rs", "m1", "t1", "m2", "t2", "den", "rden", "w1", "w2", "p1", "p2")}
        assign = sb("assign", [P, NE, TILES], BF16, r)
        inc = sb("inc", [P, NE, TILES], F32, r)
        pos = sb("pos", [P, NE, TILES], F32, r)
        reset = sb("reset", [P, NE, TILES], F32, r)
        below = sb("below", [P, P], BF16, r)
        onesb = sb("onesb", [P, P], BF16, r)
        iotas = sb("iotas", [P, NE + TILES + NBLK], I32, r)
        falling = sb("falling", [P, NE], F32, r)
        blockno = sb("blockno", [P, NBLK], F32, r)
        cnt = sb("cnt", [P, NE], F32, r)
        cnti = sb("cnti", [P, NE], I32, r)
        blocks = sb("blocks", [P, NE], F32, r)
        ones8 = sb("ones8", [P, NE], F32, r)
        ends = sb("ends", [P, NE], F32, r)
        starts = sb("starts", [P, NE], F32, r)
        cmpb = sb("cmpb", [P, NBLK, NE - 1], F32, r)
        ebf = sb("ebf", [P, NBLK], F32, r)
        place = sb("place", [P, 2, TILES], I32, r)
        r.close()

        s.update({n: sem(n) for n in """zt_in ztp z_hi z_lo wgin wsh_hi wsh_lo lgt rexp rdve rpre rios
                  wsin bsin xb2 hp silu h_hi h_lo yp ysum outst scat iot rowsready placed routed""".split()})
        ws_in = [sem(f"ws_in{i}") for i in range(2)]
        ws_views = [ws1.rearrange("(k p) n -> p k n", p=P), ws2.rearrange("(k p) n -> p k n", p=P)]
        at_assign = []
        zbanks = [bank_q, bank_k, bank_m, bank_o]

        with nc.Block() as block:
            @block.sync
            def _(sp):
                for i in range(2):
                    k = ws_views[i].shape[1]
                    sp.dma_start(stage[:, i, :].rearrange("p (k n) -> p k n", k=k), ws_views[i]).then_inc(ws_in[i], 16)
                with sp.Fori(0, G) as g:
                    sp.wait_ge(s["ysum"], 1 + 2 * g + 2)
                    sp.dma_start(out_v[:, bass.ds(g * GT, GT), :], xall[:, bass.ds(g * GT, GT), :]).then_inc(s["outst"], 16)
                sp.wait_ge(s["outst"], 16 * G)

            @block.gpsimd
            def _(pool):
                nc.gpsimd.iota(iotas[:, 0:NE], pattern=[[-1, NE]], base=NE, channel_multiplier=0).then_inc(s["iot"], 1)
                nc.gpsimd.iota(iotas[:, NE:NE + TILES], pattern=[[P, TILES]], base=0, channel_multiplier=1).then_inc(s["iot"], 1)
                nc.gpsimd.iota(iotas[:, NE + TILES:], pattern=[[1, NBLK]], base=0, channel_multiplier=0).then_inc(s["iot"], 1)
                nc.gpsimd.memset(onesb[:, :], 1.0).then_inc(s["iot"], 1)
                nc.gpsimd.memset(ones8[:, :], 1.0).then_inc(s["iot"], 1)
                nc.gpsimd.memset(reset[:, :, :], 1.0).then_inc(s["iot"], 1)
                pool.wait_ge(s["iot"], 6)
                nc.gpsimd.affine_select(out=below[:, :], in_=onesb[:, :], compare_op=ALU.is_gt, fill=0.0, base=0,
                                        pattern=[[1, P]], channel_multiplier=-1).then_inc(s["iot"], 1)
                nc.gpsimd.memset(reset[:, :, 0:1], 0.0).then_inc(s["iot"], 1)
                for i in range(2):
                    pool.wait_ge(s["wsh_hi"], i + 1)
                    nc.gpsimd.tensor_tensor(wt_lo[:, i, :], stage[:, i, :], wt_hi[:, i, :].bitcast(F32),
                                            ALU.subtract).then_inc(s["wsh_lo"], 1)
                pool.wait_ge(s["placed"], 1)
                for t in range(TILES):
                    for c in range(2):
                        nc.gpsimd.indirect_dma_start(
                            out=slots, out_offset=bass.IndirectOffsetOnAxis(ap=place[:, c, t:t + 1].bitcast(U32), axis=0),
                            in_=xrows[:, t, :], in_offset=None).then_inc(s["scat"], 16)
                pool.wait_ge(s["scat"], 2 * TILES * 16)

            @block.scalar
            def _(act):
                count_from_one(act, "silu")
                act.dma_start(wg_raw[:, :, :], wg.rearrange("(k p) n -> p k n", p=P)).then_inc(s["wgin"], 16)
                act.dma_start(bs1c[:, :], bs1.rearrange("(a p) -> p a", p=P), allow_slow_non_contiguous=True).then_inc(s["bsin"], 16)
                act.dma_start(bs2_bc[:, :], bs2.rearrange("(a n) -> a n", a=1).broadcast_to([P, C])).then_inc(s["bsin"], 16)
                act.wait_ge(s["wgin"], 16)
                nc.scalar.activation(wg_hi[:, :, :], wg_raw[:, :, :], ACT.Copy).then_inc(s["wgin"], 1)
                for j in range(G * KC):
                    act.wait_ge(s["ztp"], j + 1)
                    nc.scalar.activation(zT_hi[:, j % KC, (j // KC) * GW:(j // KC + 1) * GW], zbanks[j % 4][:, :], ACT.Copy).then_inc(s["z_hi"], 1)
                for i in range(2):
                    act.wait_ge(ws_in[i], 16)
                    nc.scalar.activation(wt_hi[:, i, :], stage[:, i, :], ACT.Copy).then_inc(s["wsh_hi"], 1)
                act.wait_ge(s["rdve"], 2)
                nc.scalar.activation(rt["p"][:, :, :], rt["d"][:, :, :], ACT.Exp).then_inc(s["rexp"], 1)
                act.wait_ge(s["bsin"], 32)
                with act.Fori(0, G) as g:
                    for f in range(NF):
                        n = g * NF + f
                        act.wait_ge(s["hp"], n + 1)
                        act.wait_ge(s["h_lo"], 1 + (n - 1 if f else g * NF))
                        nc.scalar.activation(sh[:, f % 2, :], bank_s[f % 2][:, :], ACT.Silu, bias=bs1c[:, f:f + 1]).then_inc(s["silu"], 1)
                        act.wait_ge(s["silu"], 1 + n + 1)
                        if f == 0:
                            act.wait_ge(s["yp"], 1 + 2 * g)
                        nc.scalar.activation(hT_hi[:, f, :], sh[:, f % 2, :], ACT.Copy).then_inc(s["h_hi"], 1)

            @block.vector
            def _(dve):
                count_from_one(dve, "h_lo ysum")
                steps = [0]

                def link(ins):
                    steps[0] += 1
                    ins.then_inc(s["rdve"], 1)
                    dve.wait_ge(s["rdve"], steps[0])

                def over(v, n):
                    return v.rearrange("p (t a) -> p t a", a=1).broadcast_to([P, v.shape[1], n])

                dve.wait_ge(s["wgin"], 17)
                nc.vector.tensor_tensor(wg_lo[:, :, :], wg_raw[:, :, :], wg_hi[:, :, :].bitcast(F32), ALU.subtract).then_inc(s["wgin"], 1)
                for j in range(G * KC):
                    dve.wait_ge(s["z_hi"], j + 1)
                    c = slice((j // KC) * GW, (j // KC + 1) * GW)
                    nc.vector.tensor_tensor(zT_lo[:, j % KC, c], zbanks[j % 4][:, :], zT_hi[:, j % KC, c].bitcast(F32), ALU.subtract).then_inc(s["z_lo"], 1)
                lg = bank_t[0][:, 0:TE].rearrange("p (t e) -> p t e", e=NE)
                dve.wait_ge(s["lgt"], 1)
                link(nc.vector.tensor_reduce(rm["m"][:, :], lg, AX.X, ALU.max))
                link(nc.vector.tensor_tensor(rt["d"][:, :, :], lg, over(rm["m"][:, :], NE), ALU.subtract))
                dve.wait_ge(s["rexp"], 1)
                link(nc.vector.tensor_reduce(rm["sum"][:, :], rt["p"][:, :, :], AX.X, ALU.add))
                link(nc.vector.reciprocal(rm["rs"][:, :], rm["sum"][:, :]))
                link(nc.vector.tensor_tensor(rt["p"][:, :, :], rt["p"][:, :, :], over(rm["rs"][:, :], NE), ALU.mult))
                dve.wait_ge(s["iot"], 8)
                link(nc.vector.tensor_copy(falling[:, :], iotas[:, 0:NE]))
                link(nc.vector.tensor_copy(xrows[:, :, C].bitcast(I32), iotas[:, NE:NE + TILES]))
                link(nc.vector.tensor_copy(blockno[:, :], iotas[:, NE + TILES:]))
                fall = falling[:, :].rearrange("p (a e) -> p a e", a=1).broadcast_to([P, TILES, NE])

                def pick(prob, m, t, oh):
                    link(nc.vector.tensor_reduce(m, prob, AX.X, ALU.max))
                    link(nc.vector.tensor_tensor(rt["eq"][:, :, :], prob, over(m, NE), ALU.is_equal))
                    link(nc.vector.tensor_tensor(rt["eq"][:, :, :], rt["eq"][:, :, :], fall, ALU.mult))
                    link(nc.vector.tensor_reduce(t, rt["eq"][:, :, :], AX.X, ALU.max))
                    link(nc.vector.tensor_tensor(oh, fall, over(t, NE), ALU.is_equal))
                pick(rt["p"][:, :, :], rm["m1"][:, :], rm["t1"][:, :], rt["oh1"][:, :, :])
                link(nc.vector.scalar_tensor_tensor(out=rt["p2"][:, :, :], in0=rt["oh1"][:, :, :], scalar=-2.0,
                                                    in1=rt["p"][:, :, :], op0=ALU.mult, op1=ALU.add))
                pick(rt["p2"][:, :, :], rm["m2"][:, :], rm["t2"][:, :], rt["oh2"][:, :, :])
                link(nc.vector.tensor_tensor(assign[:, :, :].rearrange("p e t -> p t e"), rt["oh1"][:, :, :], rt["oh2"][:, :, :], ALU.add))
                at_assign.append(steps[0])
                link(nc.vector.scalar_tensor_tensor(out=rm["den"][:, :], in0=rm["m1"][:, :], scalar=1e-9,
                                                    in1=rm["m2"][:, :], op0=ALU.add, op1=ALU.add))
                link(nc.vector.reciprocal(rm["rden"][:, :], rm["den"][:, :]))
                link(nc.vector.tensor_tensor(rm["w1"][:, :], rm["m1"][:, :], rm["rden"][:, :], ALU.mult))
                link(nc.vector.tensor_tensor(rm["w2"][:, :], rm["m2"][:, :], rm["rden"][:, :], ALU.mult))
                link(nc.vector.tensor_tensor(rt["eq"][:, :, :], rt["oh1"][:, :, :], over(rm["w1"][:, :], NE), ALU.mult))
                link(nc.vector.tensor_tensor(rt["tmp"][:, :, :], rt["oh2"][:, :, :], over(rm["w2"][:, :], NE), ALU.mult))
                link(nc.vector.tensor_tensor(xrows[:, :, C + 1:C + 1 + NE], rt["eq"][:, :, :], rt["tmp"][:, :, :], ALU.add))
                dve.wait_ge(s["rpre"], 1)
                pre = bank_t[1][:, 0:TE].rearrange("p (e t) -> p e t", t=TILES)
                tot = bank_t[1][:, TE:2 * TE].rearrange("p (e t) -> p e t", t=TILES)
                flat1 = lambda v: v.rearrange("p e t -> p (e t)")
                link(nc.vector.tensor_tensor_scan(flat1(inc[:, :, :]), flat1(reset[:, :, :]), bank_t[1][:, TE:2 * TE], 0.0, ALU.mult, ALU.add))
                link(nc.vector.tensor_scalar(cnti[:, :], inc[:, :, TILES - 1], float(P - 1), None, ALU.add))
                link(nc.vector.tensor_scalar(cnti[:, :], cnti[:, :], 7, None, ALU.arith_shift_right))
                link(nc.vector.tensor_copy(blocks[:, :], cnti[:, :]))
                link(nc.vector.tensor_tensor_scan(ends[:, :], ones8[:, :], blocks[:, :], 0.0, ALU.mult, ALU.add))
                link(nc.vector.tensor_tensor(starts[:, :], ends[:, :], blocks[:, :], ALU.subtract))
                link(nc.vector.tensor_tensor(pos[:, :, :], inc[:, :, :], tot, ALU.subtract))
                link(nc.vector.tensor_tensor(pos[:, :, :], pos[:, :, :], pre, ALU.add))
                link(nc.vector.scalar_tensor_tensor(out=pos[:, :, :], in0=over(starts[:, :], TILES), scalar=float(P),
                                                    in1=pos[:, :, :], op0=ALU.mult, op1=ALU.add))
                for c in range(2):
                    link(nc.vector.tensor_tensor(rt["tmp"][:, :, :], rt[("oh1", "oh2")[c]][:, :, :],
                                                 pos[:, :, :].rearrange("p e t -> p t e"), ALU.mult))
                    link(nc.vector.tensor_reduce(rm[("p1", "p2")[c]][:, :], rt["tmp"][:, :, :], AX.X, ALU.add))
                    link(nc.vector.tensor_copy(place[:, c, :], rm[("p1", "p2")[c]][:, :]))
                nc.vector.tensor_copy(startsi[:, :], starts[:, :]).then_inc(s["placed"], 1)
                link(nc.vector.tensor_tensor(cmpb[:, :, :], over(blockno[:, :], NE - 1),
                                             starts[:, 1:NE].rearrange("p (a e) -> p a e", a=1).broadcast_to([P, NBLK, NE - 1]), ALU.is_ge))
                link(nc.vector.tensor_reduce(ebf[:, :], cmpb[:, :, :], AX.X, ALU.add))
                link(nc.vector.tensor_copy(ebi[:, 0, :], ebf[:, :]))
                link(nc.vector.tensor_scalar(ebi[:, 1, :], ebi[:, 0, :], 1, None, ALU.bitwise_and))
                dve.wait_ge(s["bsin"], 32)
                nc.vector.tensor_scalar(bs2_bc[:, :], bs2_bc[:, :], SHARED, None, ALU.mult).then_inc(s["xb2"], 1)
                dve.wait_ge(s["xb2"], 1)
                for g in range(G):
                    nc.vector.tensor_tensor(xall[:, g * GT:(g + 1) * GT, :], xall[:, g * GT:(g + 1) * GT, :],
                                            bs2_bc[:, :].rearrange("p (a c) -> p a c", a=1).broadcast_to([P, GT, C]),
                                            ALU.add).then_inc(s["xb2"], 1)
                dve.wait_ge(s["xb2"], 1 + G)
                with dve.Fori(0, G) as g:
                    for f in range(NF):
                        dve.wait_ge(s["h_hi"], g * NF + f + 1)
                        nc.vector.tensor_tensor(hT_lo[:, f, :], sh[:, f % 2, :], hT_hi[:, f, :].bitcast(F32), ALU.subtract).then_inc(s["h_lo"], 1)
                    for h in range(2):
                        dve.wait_ge(s["yp"], 1 + 2 * g + h + 1)
                        xa = xall[:, bass.ds(g * GT + 2 * h, 2), :].rearrange("p t c -> p (t c)")
                        nc.vector.scalar_tensor_tensor(out=xa, in0=(bank_m, bank_o)[h][:, :], scalar=SHARED, in1=xa,
                                                       op0=ALU.mult, op1=ALU.add).then_inc(s["ysum"], 1)

            @block.tensor
            def _(pe):
                count_from_one(pe, "yp")
                for j in range(G * KC):
                    k, c = j % KC, j // KC
                    if j >= 4:
                        pe.wait_ge(s["z_lo"], j - 3)
                    for t in range(GT):
                        last = nc.tensor.transpose(zbanks[j % 4][:, t * P:(t + 1) * P], xrows[:, c * GT + t, k * P:(k + 1) * P], ident[:, :])
                    last.then_inc(s["ztp"], 1)
                pe.wait_ge(s["z_lo"], G * KC)
                pe.wait_ge(s["wgin"], 18)
                for t in range(TILES):
                    for k in range(KC):
                        last = three(pe, bank_t[0][:, t * NE:(t + 1) * NE], lambda lo: (zT_lo if lo else zT_hi)[:, k, t * P:(t + 1) * P],
                                     lambda lo: (wg_lo if lo else wg_hi)[:, k, :], k == 0, k == KC - 1)
                last.then_inc(s["lgt"], 1)

                def prefix():
                    pe.wait_ge(s["iot"], 8)
                    pe.wait_ge(s["rdve"], at_assign[0])
                    a = assign[:, :, :].rearrange("p e t -> p (e t)")
                    nc.tensor.matmul(bank_t[1][:, 0:TE], below[:, :], a, start=True, stop=True)
                    nc.tensor.matmul(bank_t[1][:, TE:2 * TE], onesb[:, :], a, start=True, stop=True).then_inc(s["rpre"], 1)
                prefix()
                pe.wait_ge(s["wsh_lo"], 2)
                with pe.Fori(0, G) as g:
                    for f in range(NF):
                        n = g * NF + f
                        pe.wait_ge(s["silu"], 1 + (n - 1 if f else g * NF))
                        for k in range(KC):
                            last = three(pe, bank_s[f % 2][:, :], lambda lo: w_of(0, lo, ws_views[0])[:, k, f * P:(f + 1) * P],
                                         lambda lo: (zT_lo if lo else zT_hi)[:, k, bass.ds(g * GW, GW)], k == 0, k == KC - 1)
                        last.then_inc(s["hp"], 1)
                    pe.wait_ge(s["h_lo"], 1 + (g + 1) * NF)
                    for h in range(2):
                        pe.wait_ge(s["ysum"], 1 + 2 * g)
                        for t in range(2):
                            for f in range(NF):
                                q = slice((2 * h + t) * P, (2 * h + t + 1) * P)
                                last = three(pe, (bank_m, bank_o)[h][:, t * C:(t + 1) * C], lambda lo: (hT_lo if lo else hT_hi)[:, f, q],
                                             lambda lo: w_of(1, lo, ws_views[1])[:, f, :], f == 0, f == NF - 1)
                        last.then_inc(s["yp"], 1)

        U = 4
        e_ = ExitStack()
        we1 = sb("we1", [P, 2, KC, F], F32, e_)
        we2 = sb("we2", [P, 2, NF, C], F32, e_)
        b1_bc = sb("b1_bc", [P, 2, F], F32, e_)
        b2_bc = sb("b2_bc", [P, NE, C], F32, e_)
        xs = sb("xs", [P, U, ROW], F32, e_)
        xsT = sb("xsT", [P, 2, KC, P], F32, e_)
        hb = sb("hb", [P, 2, F], F32, e_)
        hbT = sb("hbT", [P, NF, P], F32, e_)
        yb = sb("yb", [P, 2, C], F32, e_)
        nop = sb("nop", [P, 1], F32, e_)
        nop_to = sb("nop_to", [P, 1], F32, e_)
        yw = sb("yw", [P, 2, C], F32, e_)
        e_.close()
        s.update({n: sem(n) for n in "b2in we_in we_ready xsT_p xsT_c g1 hbias hsilu hT_p hTc_act hTc_dve g2 yadd yw_s added nopped".split()})
        xs_in = [sem(f"xs_in{i}") for i in range(U)]
        bank_h, bank_x, bank_y, bank_hT = bank_s, bank_q, bank_m, bank_t
        LOOP = (NBLK - 3) // U

        def steps(eng, step):
            with eng.Fori(0, LOOP) as j:
                for u in range(U):
                    step(U * j + u, u, U, j)
            for i in range(U * LOOP, NBLK):
                step(i, i % U, NBLK - 1 - i, i // U)

        with nc.Block() as block:
            @block.sync
            def _(sp):
                sp.dma_start(b2_bc[:, :, :], b2.rearrange("(a e) c -> a e c", a=1).broadcast_to([P, NE, C])).then_inc(s["b2in"], 16)
                for e in range(NE):
                    if e >= 2:
                        sp.wait_ge(s["g2"], 1 + sp.value_load(startsi[0:1, e - 1:e], min_val=0, max_val=NBLK))
                    sp.dma_start(we1[:, e % 2, :, :], w1[e].rearrange("(k p) n -> p k n", p=P)).then_inc(s["we_in"], 16)
                    sp.dma_start(we2[:, e % 2, :, :], w2[e].rearrange("(k p) n -> p k n", p=P)).then_inc(s["we_in"], 16)
                    sp.dma_start(b1_bc[:, e % 2, :], b1[e:e + 1, :].broadcast_to([P, F])).then_inc(s["we_in"], 16)
                    sp.wait_ge(s["we_in"], 48 * (e + 1))
                    sp.sem_inc(s["we_ready"], 1)

            @block.gpsimd
            def _(pool):
                nc.gpsimd.memset(nop[:, :], 0.0).then_inc(s["nopped"], 1)
                pool.wait_ge(s["nopped"], 1)
                pool.dma_start(nop_to[:, :], nop[:, :]).then_inc(s["added"], 16)
                last_token = pool.to_reg(B * S - 1)

                def step(i, u, left, turn):
                    pool.wait_ge(s["yw_s"], i + 1)
                    pool.wait_ge(s["added"], 16 * (i + 1))
                    pool.wait_ge(s["nopped"], i + 1)
                    nc.gpsimd.tensor_tensor(nop[:, :], nop[:, :], nop[:, :], ALU.add).then_inc(s["nopped"], 1)
                    nc.gpsimd.indirect_dma_start(
                        out=out_f, out_offset=bass.IndirectOffsetOnAxis(ap=xs[:, u, C:C + 1].bitcast(U32), axis=0),
                        in_=yw[:, u % 2, :], in_offset=None, bounds_check=last_token, oob_is_err=False,
                        compute_op=ALU.add).then_inc(s["added"], 16)
                steps(pool, step)
                pool.wait_ge(s["added"], 16 * (NBLK + 1))

            @block.scalar
            def _(act):
                count_from_one(act, "hTc_act")
                def load(i, u):
                    act.dma_start(xs[:, u, :], slots[bass.ds(i * P, P), :]).then_inc(xs_in[u], 16)

                def silu(i, u):
                    for h in range(2):
                        act.wait_ge(s["hbias"], 2 * i + h + 1)
                        hv = hb[:, u % 2, h * 512:(h + 1) * 512]
                        nc.scalar.activation(hv, hv, ACT.Silu).then_inc(s["hsilu"], 1)

                def rows_t(i, u):
                    act.wait_ge(s["xsT_p"], i + 1)
                    nc.scalar.activation(xsT[:, u % 2, :, :], bank_x[:, 0:KC * P], ACT.Copy).then_inc(s["xsT_c"], 1)

                def step(i, u, left, turn):
                    act.wait_ge(s["hT_p"], 2 * i + 1)
                    nc.scalar.activation(hbT[:, 0:NF // 2, :], bank_hT[0][:, :], ACT.Copy).then_inc(s["hTc_act"], 1)
                    if left >= 1:
                        silu(i + 1, u + 1)
                    if left >= 2:
                        rows_t(i + 2, u + 2)
                    if left >= 3:
                        act.wait_ge(s["added"], 16 * (i + 1))
                        load(i + 3, (u + 3) % U)
                for i in range(3):
                    load(i, i)
                rows_t(0, 0)
                silu(0, 0)
                rows_t(1, 1)
                steps(act, step)

            @block.vector
            def _(dve):
                count_from_one(dve, "hTc_dve yadd")
                def bias(i, u):
                    slot = dve.value_load(ebi[0:1, 1, bass.ds(i, 1)], min_val=0, max_val=1)
                    for h in range(2):
                        dve.wait_ge(s["g1"], 2 * i + h + 1)
                        nc.vector.tensor_tensor(hb[:, u % 2, h * 512:(h + 1) * 512], bank_h[h][:, :],
                                                b1_bc[:, bass.ds(slot, 1), h * 512:(h + 1) * 512].rearrange("p a n -> p (a n)"),
                                                ALU.add).then_inc(s["hbias"], 1)

                def step(i, u, left, turn):
                    dve.wait_ge(s["hT_p"], 2 * i + 2)
                    nc.vector.tensor_copy(hbT[:, NF // 2:, :].rearrange("p f q -> p (f q)"), bank_hT[1][:, :]).then_inc(s["hTc_dve"], 1)
                    if left >= 1:
                        bias(i + 1, u + 1)
                    e = dve.value_load(ebi[0:1, 0, bass.ds(i, 1)], min_val=0, max_val=NE - 1)
                    dve.wait_ge(s["g2"], 1 + i + 1)
                    nc.vector.tensor_tensor(yb[:, u % 2, :], bank_y[:, 0:C], b2_bc[:, bass.ds(e, 1), :].rearrange("p a c -> p (a c)"),
                                            ALU.add).then_inc(s["yadd"], 1)
                    dve.wait_ge(s["added"], 16 * (i + 1))
                    dve.wait_ge(s["yadd"], 1 + i + 1)
                    nc.vector.tensor_scalar(yw[:, u % 2, :], yb[:, u % 2, :], xs[:, u, bass.ds(e + (C + 1), 1)], None,
                                            ALU.mult).then_inc(s["yw_s"], 1)
                dve.wait_ge(s["b2in"], 16)
                bias(0, 0)
                steps(dve, step)

            @block.tensor
            def _(pe):
                count_from_one(pe, "g2")
                def rows_t(i, u, at):
                    pe.wait_ge(xs_in[u], 16 * (at + 1))
                    pe.wait_ge(s["xsT_c"], i)
                    for k in range(KC):
                        last = nc.tensor.transpose(bank_x[:, k * P:(k + 1) * P], xs[:, u, k * P:(k + 1) * P], ident[:, :])
                    last.then_inc(s["xsT_p"], 1)

                def up(i, u):
                    e = pe.value_load(ebi[0:1, 0, bass.ds(i, 1)], min_val=0, max_val=NE - 1)
                    slot = pe.value_load(ebi[0:1, 1, bass.ds(i, 1)], min_val=0, max_val=1)
                    pe.wait_ge(s["we_ready"], e + 1)
                    pe.wait_ge(s["xsT_c"], i + 1)
                    for h in range(2):
                        pe.wait_ge(s["hbias"], 2 * i)
                        for k in range(KC):
                            last = nc.tensor.matmul(bank_h[h][:, :], xsT[:, u % 2, k, :],
                                                    we1[:, bass.ds(slot, 1), k, h * 512:(h + 1) * 512].rearrange("p a n -> p (a n)"),
                                                    start=k == 0, stop=k == KC - 1)
                        last.then_inc(s["g1"], 1)

                def step(i, u, left, turn):
                    pe.wait_ge(s["hTc_act"], 1 + i)
                    pe.wait_ge(s["hTc_dve"], 1 + i)
                    for h in range(2):
                        pe.wait_ge(s["hsilu"], 2 * i + h + 1)
                        for f in range(NF // 2):
                            o = (h * NF // 2 + f) * P
                            last = nc.tensor.transpose(bank_hT[h][:, f * P:(f + 1) * P], hb[:, u % 2, o:o + P], ident[:, :])
                        last.then_inc(s["hT_p"], 1)
                    if left >= 1:
                        up(i + 1, u + 1)
                    if left >= 2:
                        rows_t(i + 2, (u + 2) % U, turn + (u + 2) // U)
                    slot = pe.value_load(ebi[0:1, 1, bass.ds(i, 1)], min_val=0, max_val=1)
                    pe.wait_ge(s["hTc_act"], 1 + i + 1)
                    pe.wait_ge(s["hTc_dve"], 1 + i + 1)
                    pe.wait_ge(s["yadd"], 1 + i)
                    for f in range(NF):
                        last = nc.tensor.matmul(bank_y[:, 0:C], hbT[:, f, :], we2[:, bass.ds(slot, 1), f, :].rearrange("p a c -> p (a c)"),
                                                start=f == 0, stop=f == NF - 1)
                    last.then_inc(s["g2"], 1)
                rows_t(0, 0, 0)
                up(0, 0)
                rows_t(1, 1, 0)
                steps(pe, step)


_INS = ['x', 'ctx_1024', 'mask_BxSxS2_bk1'] + ['L0_xattn_' + n for n in ('Wq', 'bq', 'Wk', 'bk', 'Wv', 'bv', 'Wo', 'bo')] \
    + ['L0_ffn_' + n for n in ('Wg', 'W1', 'b1', 'W2', 'b2', 'Ws1', 'bs1', 'Ws2', 'bs2')]


def kernel(**inputs):
    import numpy as _np
    import concourse.bacc as _bacc
    from concourse import mybir as _mybir
    from concourse.bass_utils import run_bass_kernel_spmd as _run

    nc = _bacc.Bacc("TRN2", target_bir_lowering=False, num_devices=1)
    arrays, args = {}, []
    for name in _INS:
        a = _np.ascontiguousarray(inputs[name])
        arrays[f"in_{name}"] = a
        args.append(nc.dram_tensor(f"in_{name}", a.shape, _mybir.dt.from_np(a.dtype), kind="ExternalInput").ap())
    shape = inputs['x'].shape
    out = nc.dram_tensor("out_dram", shape, _mybir.dt.float32, kind="ExternalOutput").ap()
    xattn_moe_kernel(nc, *args, out)
    r = _run(nc, [arrays], core_ids=[0])
    return r.results[0]["out_dram"]
```

```python
import concourse.bass as bass
from concourse import mybir
from contextlib import ExitStack

F32 = mybir.dt.float32
F32R = mybir.dt.float32r
BF16 = mybir.dt.bfloat16
I32 = mybir.dt.int32
U32 = mybir.dt.uint32
U8 = mybir.dt.uint8
ALU = mybir.AluOpType
ACT = mybir.ActivationFunctionType
AX = mybir.AxisListType


def xattn_moe_kernel(nc, x, ctx_in, mask, wq, bq, wk, bk, wv, bv, wo, bo,
                     wg, w1, b1, w2, b2, ws1, bs1, ws2, bs2, out):
    B, S, C = x.shape
    SK = ctx_in.shape[1]
    HD = wq.shape[1]
    D = 64
    P = 128
    KC = C // P
    PAIRS = HD // P
    TILES = B * S // P
    GB = 2
    G = B // GB
    GT = TILES // G
    QT = S // P
    GW = GT * P
    SK2 = 2 * SK
    VW = 3 * D
    EPS = 1e-5
    SHARED = 0.1
    SCALE = D ** -0.5
    NE = wg.shape[1]
    F = w1.shape[2]
    NBLK = 2 * TILES + NE - 1
    NOBODY = B * S
    ROW = C + 9
    MASKED = -1e30

    es = ExitStack()
    with es:
        def sem(name):
            return es.enter_context(nc.semaphore(name))

        def sb(name, shape, dt, stack=es):
            return stack.enter_context(nc.sbuf_tensor(name, shape, dt))

        ident = sb("ident", [P, P], F32)
        identb = sb("identb", [P, P], BF16)
        xall = sb("xall", [P, TILES, C], F32)
        xrows = sb("xrows", [P, TILES, ROW], F32)
        wt_hi = sb("wt_hi", [P, 4, KC * HD], F32R)
        wt_lo = sb("wt_lo", [P, 4, KC * HD], F32R)
        stage = sb("stage", [P, 2, KC * HD], F32)

        startsi = sb("startsi", [P, NE], I32)
        ebi = sb("ebi", [P, 2, NBLK], I32)
        slots = nc.dram_tensor("slots", (NBLK * P, ROW), F32, kind="Internal").ap()

        a = ExitStack()
        xg = sb("xg", [P, GT, C], F32, a)
        ctxb = sb("ctxb", [SK, GB, C], F32, a)
        masku = sb("masku", [P, GT, SK], U8, a)
        maskb = sb("maskb", [P, GT, 2, SK], BF16, a)
        xT_hi = sb("xT_hi", [P, KC, GW], F32R, a)
        xT_lo = sb("xT_lo", [P, KC, GW], F32R, a)
        cT_hi = sb("cT_hi", [P, KC, GB * SK], F32R, a)
        cT_lo = sb("cT_lo", [P, KC, GB * SK], F32R, a)
        v_hi = sb("v_hi", [SK, GB, PAIRS, VW], F32R, a)
        v_lo = sb("v_lo", [SK, GB, PAIRS, VW], F32R, a)
        q_hi = sb("q_hi", [P, GW], F32R, a)
        q_lo = sb("q_lo", [P, GW], F32R, a)
        k_hi = sb("k_hi", [P, GB, SK2], F32R, a)
        k_lo = sb("k_lo", [P, GB, SK2], F32R, a)
        pT_hi = sb("pT_hi", [SK, GB, 2, QT, P], F32R, a)
        pT_lo = sb("pT_lo", [SK, GB, 2, QT, P], F32R, a)
        aT_hi = sb("aT_hi", [P, PAIRS, GW], F32R, a)
        aT_lo = sb("aT_lo", [P, PAIRS, GW], F32R, a)
        bqk = sb("bqk", [P, 3, PAIRS], F32, a)
        bo_bc = sb("bo_bc", [P, C], F32, a)
        stats = sb("stats", [P, GT, 6], F32, a)
        mv = sb("mv", [P, GT, 2], F32, a)
        rstd = sb("rstd", [P, GT], F32, a)
        fence = sb("fence", [P, 1], F32, a)
        vareps = sb("vareps", [P, GT], F32, a)
        mhalf = sb("mhalf", [P, GT], F32, a)
        epst = sb("epst", [P, GT], F32, a)
        nmax = sb("nmax", [P, 2, GT, 2], F32, a)
        ssum = sb("ssum", [P, 2, GT, 2], F32, a)
        rsum = sb("rsum", [P, 2, GT, 2], F32, a)
        a.close()

        flat = stage[:, :, :].rearrange("p a n -> p (a n)")
        x2g = flat[:, 2 * GT * SK2:2 * GT * SK2 + GT * C].rearrange("p (t c) -> p t c", t=GT)
        pad_at = 2 * GT * SK2 + GT * C
        padrow = flat[:, pad_at:pad_at + ROW]
        pr = flat[:, 0:2 * GT * SK2] \
            .rearrange("p (r t h k) -> p r t h k", r=2, t=GT, h=2)

        ps = ExitStack()

        def pb(name):
            return ps.enter_context(nc.psum_tensor(name, [P, 512], F32))
        bank_q, bank_k, bank_m, bank_o = pb("bank_q"), pb("bank_k"), pb("bank_m"), pb("bank_o")
        bank_s = [pb("bank_s0"), pb("bank_s1")]
        bank_t = [pb("bank_t0"), pb("bank_t1")]
        ps.close()

        names = """pad padded ve x2_kept bias_in bo_in bq_s xg_in mask_in ctx_in w_hi w_lo const zeros ln1 xbo xt ct
                   xt_hi xt_lo ct_hi ct_lo vp v_hi_s v_lo_s mb qk_q qk_k q_hi_s k_hi_s q_lo_s k_lo_s
                   sc mx ex rc nrm tp p_hi p_lo pv a_hi a_lo wo_d x2 ln2 dv_st dv_ag dv_rs""".split()
        s = {n: sem(n) for n in names}
        v_banks = [bank_t[0], bank_t[1], bank_m, bank_o]
        wraw_in = [sem(f"wraw_in{i}") for i in range(4)]

        x_v = x.rearrange("b (t p) c -> p (b t) c", p=P)
        m_v = mask.rearrange("b (t p) k -> p (b t) k", p=P)
        w_views = [wv.rearrange("(k p) n -> p k n", p=P), wk.rearrange("(k p) n -> p k n", p=P),
                   wq.rearrange("(k p) n -> p k n", p=P), wo.rearrange("(k p) n -> p k n", p=P)]
        ctx_v = ctx_in.rearrange("b k c -> k b c")

        def w_of(i, lo, view=None):
            return (wt_lo if lo else wt_hi)[:, i, :].rearrange("p (k n) -> p k n", n=(w_views[i] if view is None else view).shape[2])

        def count_from_one(eng, names):
            for n in names.split():
                eng.sem_inc(s[n], 1)

        def three(pe, o, st, mo, first, last):
            nc.tensor.matmul(o, st(0), mo(0), start=first, stop=False)
            nc.tensor.matmul(o, st(0), mo(1), start=False, stop=False)
            return nc.tensor.matmul(o, st(1), mo(0), start=False, stop=last)

        with nc.Block() as block:
            @block.sync
            def _(sp):
                def load_weight(i):
                    k = w_views[i].shape[1]
                    sp.dma_start(stage[:, i % 2, :].rearrange("p (k n) -> p k n", k=k), w_views[i]).then_inc(wraw_in[i], 16)
                sp.dma_start(xg[:, :, :], x_v[:, 0:GT, :]).then_inc(s["xg_in"], 16)
                sp.dma_start(ctxb[:, :, :], ctx_v[:, 0:GB, :]).then_inc(s["ctx_in"], 16)
                load_weight(0)
                load_weight(1)
                sp.dma_start(masku[:, :, :], m_v[:, 0:GT, :]).then_inc(s["mask_in"], 16)
                for i in (2, 3):
                    sp.wait_ge(s["w_lo"], i - 1)
                    load_weight(i)
                sp.wait_ge(s["pad"], 2)
                sp.dma_start(slots.rearrange("(b p) n -> p b n", p=P), padrow[:, :].rearrange("p (a n) -> p a n", a=1)
                             .broadcast_to([P, NBLK, ROW])).then_inc(s["padded"], 16)
                with sp.Fori(1, G) as g:
                    sp.wait_ge(s["mb"], g)
                    sp.dma_start(masku[:, :, :], m_v[:, bass.ds(g * GT, GT), :]).then_inc(s["mask_in"], 16)
                    sp.wait_ge(s["xt"], g * KC)
                    sp.dma_start(xg[:, :, :], x_v[:, bass.ds(g * GT, GT), :]).then_inc(s["xg_in"], 16)
                    sp.wait_ge(s["ct"], g)
                    sp.dma_start(ctxb[:, :, :], ctx_v[:, bass.ds(g * GB, GB), :]).then_inc(s["ctx_in"], 16)
                sp.wait_ge(s["padded"], 16)

            @block.gpsimd
            def _(pool):
                count_from_one(pool, "x2_kept")
                pool.dma_start(bo_bc[:, :], bo.rearrange("(a n) -> a n", a=1).broadcast_to([P, C])).then_inc(s["bo_in"], 16)

                def rsqrt(stat):
                    pool.wait_ge(s["dv_ag"], stat * GT + GT)
                    nc.gpsimd.tensor_tensor(vareps[:, :], mv[:, :, 1], epst[:, :], ALU.add).then_inc(s["ve"], 1)
                    pool.wait_ge(s["ve"], stat + 1)
                    nc.gpsimd.tensor_tensor(rstd[:, :], vareps[:, :], mhalf[:, :], ALU.pow).then_inc(s["dv_rs"], 1)

                def add_bo(g):
                    nc.gpsimd.tensor_tensor(xall[:, bass.ds(g * GT, GT), :], xg[:, :, :],
                                            bo_bc[:, :].rearrange("p (a c) -> p a c", a=1).broadcast_to([P, GT, C]),
                                            ALU.add).then_inc(s["xbo"], 1)

                nc.gpsimd.memset(mhalf[:, :], -0.5).then_inc(s["zeros"], 1)
                nc.gpsimd.memset(epst[:, :], EPS).then_inc(s["zeros"], 1)
                nc.gpsimd.memset(ident[:, :], 0.0).then_inc(s["zeros"], 1)
                nc.gpsimd.memset(identb[:, :], 0.0).then_inc(s["zeros"], 1)
                pool.wait_ge(s["zeros"], 4)
                for m in (ident, identb):
                    nc.gpsimd.affine_select(out=m[:, :], in_=m[:, :], compare_op=ALU.not_equal, fill=1.0, base=0,
                                            pattern=[[-1, P]], channel_multiplier=1).then_inc(s["const"], 1)
                pool.wait_ge(s["bo_in"], 16)
                pool.wait_ge(s["xg_in"], 16)
                rsqrt(0)
                add_bo(0)
                for z in (v_hi, v_lo, k_hi, k_lo):
                    nc.gpsimd.memset(z[:].bitcast(F32), 0.0).then_inc(s["const"], 1)
                pool.wait_ge(s["w_lo"], 4)
                nc.gpsimd.memset(padrow[:, :], 0.0).then_inc(s["pad"], 1)
                pool.wait_ge(s["pad"], 1)
                nc.gpsimd.memset(padrow[:, C:C + 1].bitcast(I32), NOBODY).then_inc(s["pad"], 1)

                def body(g, more):
                    for p in range(PAIRS):
                        for b in range(GB):
                            pool.wait_ge(s["rc"], (g * PAIRS + p) * GB + b + 1)
                            pt = pr[:, p % 2, b * QT:(b + 1) * QT, :, :]
                            nc.gpsimd.tensor_tensor(
                                pt, pt, rsum[:, p % 2, b * QT:(b + 1) * QT, :].rearrange("p t (h a) -> p t h a", a=1)
                                .broadcast_to([P, QT, 2, SK]), ALU.mult).then_inc(s["nrm"], 1)
                        if more and p == 2:
                            rsqrt(2 * g + 1)
                            add_bo(g + 1)
                    pool.wait_ge(s["x2"], 1 + g * 2 + 2)
                    nc.gpsimd.tensor_copy(xall[:, bass.ds(g * GT, GT), :], x2g).then_inc(s["x2_kept"], 1)
                    rsqrt(2 * g + (2 if more else 1))
                with pool.Fori(0, G - 1) as g:
                    body(g, True)
                body(G - 1, False)

            @block.scalar
            def _(act):
                count_from_one(act, "ex")
                for i, bb in enumerate((bq, bk, bv)):
                    act.dma_start(bqk[:, i, :], bb.rearrange("(a p) -> p a", p=P), allow_slow_non_contiguous=True).then_inc(s["bias_in"], 16)

                def split_weight(i):
                    act.wait_ge(wraw_in[i], 16)
                    nc.scalar.activation(wt_hi[:, i, :], stage[:, i % 2, :], ACT.Copy, scale=SCALE if i == 2 else 1.0).then_inc(s["w_hi"], 1)

                def transposed(g):
                    for k in range(KC):
                        act.wait_ge(s["xt"], g * KC + k + 1)
                        nc.scalar.activation(xT_hi[:, k, :], (bank_q, bank_k)[k][:, :], ACT.Copy).then_inc(s["xt_hi"], 1)
                    act.wait_ge(s["ct"], g + 1)
                    nc.scalar.activation(cT_hi[:, :, :], bank_m[:, 0:KC * GB * SK], ACT.Copy).then_inc(s["ct_hi"], 1)

                def values_hi(g):
                    for j in range(2 * GB):
                        act.wait_ge(s["vp"], g * 2 * GB + j + 1)
                        b, h = j // 2, j % 2
                        vin = v_banks[j][0:SK, :].rearrange("p (a e d) -> p a e d", e=2, d=D)
                        vout = v_hi[:, b, h * PAIRS // 2:(h + 1) * PAIRS // 2, :] \
                            .rearrange("p a (e d) -> p a e d", d=D)[:, :, 0:3:2, :]
                        nc.scalar.activation(vout, vin, ACT.Copy).then_inc(s["v_hi_s"], 1)

                def qk_hi(n, p):
                    act.wait_ge(s["qk_q"], n + 1)
                    act.wait_ge(s["sc"], 1 + n * GB)
                    nc.scalar.activation(q_hi[:, :], bank_q[:, :], ACT.Identity, bias=bqk[:, 0, p:p + 1]).then_inc(s["q_hi_s"], 1)
                    act.wait_ge(s["qk_k"], n + 1)
                    for e in range(2):
                        r = slice(e * D, (e + 1) * D)
                        nc.scalar.activation(k_hi[r, :, e * SK:(e + 1) * SK],
                                             bank_k[r, 0:GB * SK].rearrange("p (b k) -> p b k", b=GB),
                                             ACT.Identity, bias=bqk[r, 1, p:p + 1]).then_inc(s["k_hi_s"], 1)

                def exps(n, p, b):
                    act.wait_ge(s["tp"], 1 + ((n - 1) * GB if p else n * GB))
                    act.wait_ge(s["mx"], n * GB + b + 1)
                    for t in range(QT):
                        for h in range(2):
                            o = (t * 2 + h) * SK
                            st = (slice(None), p % 2, b * QT + t, slice(h, h + 1))
                            last = nc.scalar.activation(pr[:, p % 2, b * QT + t, h, :], bank_s[b][:, o:o + SK], ACT.Exp,
                                                        bias=nmax[st], accum_out=ssum[st])
                    last.then_inc(s["ex"], 1)

                def pt_hi(n):
                    for b in range(GB):
                        act.wait_ge(s["tp"], 1 + n * GB + b + 1)
                        act.wait_ge(s["pv"], 1 + n)
                        nc.scalar.activation(pT_hi[:, b, :, :, :], bank_t[b][0:SK, :], ACT.Copy).then_inc(s["p_hi"], 1)

                def a_hi(g, n, p):
                    act.wait_ge(s["pv"], 1 + n + 1)
                    if p == 0:
                        act.wait_ge(s["wo_d"], 1 + g * 2)
                    nc.scalar.activation(aT_hi[:, p, :], bank_o[:, :], ACT.Identity, bias=bqk[:, 2, p:p + 1]).then_inc(s["a_hi"], 1)

                split_weight(0)
                act.wait_ge(s["const"], 4)
                transposed(0)
                split_weight(1)
                values_hi(0)
                split_weight(2)
                act.wait_ge(s["bias_in"], 48)
                act.wait_ge(s["bq_s"], 1)
                act.wait_ge(s["const"], 6)
                qk_hi(0, 0)
                split_weight(3)

                def body(g, more):
                    for p in range(PAIRS):
                        n = g * PAIRS + p
                        exps(n, p, 0)
                        if p:
                            pt_hi(n - 1)
                        exps(n, p, 1)
                        if p + 1 < PAIRS:
                            qk_hi(n + 1, p + 1)
                        if p:
                            a_hi(g, n - 1, p - 1)
                    n = (g + 1) * PAIRS
                    if more:
                        transposed(g + 1)
                    pt_hi(n - 1)
                    a_hi(g, n - 1, PAIRS - 1)
                    if more:
                        values_hi(g + 1)
                        qk_hi(n, 0)
                with act.Fori(0, G - 1) as g:
                    body(g, True)
                body(G - 1, False)

            @block.vector
            def _(dve):
                count_from_one(dve, "x2 p_lo a_lo q_lo_s k_lo_s")

                def statistics(tile, stat):
                    for t in range(GT):
                        nc.vector.bn_stats(stats[:, t, :], tile(t)).then_inc(s["dv_st"], 1)
                    dve.wait_ge(s["dv_st"], stat * GT + GT)
                    nc.vector.memset(fence[:, :], 0.0)
                    for t in range(GT):
                        nc.vector.bn_aggr(mv[:, t, :], stats[:, t, :]).then_inc(s["dv_ag"], 1)

                def normalize(tile, done, stat, dst):
                    dve.wait_ge(s["dv_rs"], stat + 1)
                    for t in range(GT):
                        last = nc.vector.tensor_scalar(dst(t), tile(t), mv[:, t, 0:1], rstd[:, t:t + 1],
                                                       ALU.subtract, ALU.mult)
                    last.then_inc(s[done], 1)

                def weight_lo(i):
                    dve.wait_ge(s["w_hi"], i + 1)
                    nc.vector.scalar_tensor_tensor(out=wt_lo[:, i, :], in0=stage[:, i % 2, :], scalar=SCALE if i == 2 else 1.0,
                                                   in1=wt_hi[:, i, :].bitcast(F32), op0=ALU.mult, op1=ALU.subtract).then_inc(s["w_lo"], 1)

                def add_mask(g):
                    dve.wait_ge(s["sc"], 1 + g * PAIRS * GB)
                    dve.wait_ge(s["mask_in"], 16 * (g + 1))
                    nc.vector.tensor_scalar(maskb[:, :, :, :], masku[:, :, :]
                                            .rearrange("p t (a k) -> p t a k", a=1).broadcast_to([P, GT, 2, SK]),
                                            MASKED, None, ALU.mult).then_inc(s["mb"], 1)

                def transposed(g):
                    for k in range(KC):
                        dve.wait_ge(s["xt_hi"], g * KC + k + 1)
                        nc.vector.tensor_tensor(xT_lo[:, k, :], (bank_q, bank_k)[k][:, :], xT_hi[:, k, :].bitcast(F32),
                                                ALU.subtract).then_inc(s["xt_lo"], 1)
                    dve.wait_ge(s["ct_hi"], g + 1)
                    nc.vector.tensor_tensor(cT_lo[:, :, :].rearrange("p k n -> p (k n)"), bank_m[:, 0:KC * GB * SK],
                                            cT_hi[:, :, :].bitcast(F32).rearrange("p k n -> p (k n)"),
                                            ALU.subtract).then_inc(s["ct_lo"], 1)

                def values_lo(g):
                    for j in range(2 * GB):
                        dve.wait_ge(s["v_hi_s"], g * 2 * GB + j + 1)
                        b, h = j // 2, j % 2
                        vin = v_banks[j][0:SK, :].rearrange("p (a e d) -> p a e d", e=2, d=D)
                        sel = lambda v: v[:, b, h * PAIRS // 2:(h + 1) * PAIRS // 2, :] \
                            .rearrange("p a (e d) -> p a e d", d=D)[:, :, 0:3:2, :]
                        nc.vector.tensor_tensor(sel(v_lo), vin, sel(v_hi).bitcast(F32), ALU.subtract).then_inc(s["v_lo_s"], 1)

                def qk_lo(n, p):
                    dve.wait_ge(s["q_hi_s"], n + 1)
                    nc.vector.scalar_tensor_tensor(out=q_lo[:, :], in0=bank_q[:, :], scalar=bqk[:, 0, p:p + 1],
                                                   in1=q_hi[:, :].bitcast(F32), op0=ALU.add, op1=ALU.subtract).then_inc(s["q_lo_s"], 1)
                    dve.wait_ge(s["k_hi_s"], 2 * (n + 1))
                    for e in range(2):
                        r = slice(e * D, (e + 1) * D)
                        nc.vector.scalar_tensor_tensor(
                            out=k_lo[r, :, e * SK:(e + 1) * SK],
                            in0=bank_k[r, 0:GB * SK].rearrange("p (b k) -> p b k", b=GB), scalar=bqk[r, 1, p:p + 1],
                            in1=k_hi[r, :, e * SK:(e + 1) * SK].bitcast(F32), op0=ALU.add, op1=ALU.subtract).then_inc(s["k_lo_s"], 1)

                def maxima(n, p):
                    for b in range(GB):
                        dve.wait_ge(s["sc"], 1 + n * GB + b + 1)
                        sc = bank_s[b][:, 0:QT * SK2].rearrange("p (t h k) -> p t h k", t=QT, h=2)
                        nc.vector.tensor_reduce(nmax[:, p % 2, b * QT:(b + 1) * QT, :], sc, AX.X, ALU.max,
                                                negate=True).then_inc(s["mx"], 1)

                def reciprocals(n, p, b):
                    dve.wait_ge(s["ex"], 1 + n * GB + b + 1)
                    nc.vector.reciprocal(rsum[:, p % 2, b * QT:(b + 1) * QT, :],
                                         ssum[:, p % 2, b * QT:(b + 1) * QT, :]).then_inc(s["rc"], 1)

                def pt_lo(n):
                    for b in range(GB):
                        dve.wait_ge(s["p_hi"], n * GB + b + 1)
                        nc.vector.tensor_tensor(pT_lo[:, b, :, :, :].rearrange("p h t q -> p (h t q)"), bank_t[b][0:SK, :],
                                                pT_hi[:, b, :, :, :].bitcast(F32).rearrange("p h t q -> p (h t q)"),
                                                ALU.subtract).then_inc(s["p_lo"], 1)

                def a_lo(n, p):
                    dve.wait_ge(s["a_hi"], n + 1)
                    nc.vector.scalar_tensor_tensor(out=aT_lo[:, p, :], in0=bank_o[:, :], scalar=bqk[:, 2, p:p + 1],
                                                   in1=aT_hi[:, p, :].bitcast(F32), op0=ALU.add, op1=ALU.subtract).then_inc(s["a_lo"], 1)

                dve.wait_ge(s["xg_in"], 16)
                statistics(lambda t: xg[:, t, :], 0)
                dve.wait_ge(s["xbo"], 1)
                normalize(lambda t: xg[:, t, :], "ln1", 0, lambda t: xg[:, t, :])
                weight_lo(0)
                dve.wait_ge(s["const"], 6)
                transposed(0)
                weight_lo(1)
                values_lo(0)
                dve.wait_ge(s["bias_in"], 48)
                nc.vector.tensor_scalar(bqk[:, 0, :], bqk[:, 0, :], SCALE, None, ALU.mult).then_inc(s["bq_s"], 1)
                weight_lo(2)
                dve.wait_ge(s["bq_s"], 1)
                qk_lo(0, 0)
                add_mask(0)
                weight_lo(3)

                def body(g, more):
                    for p in range(PAIRS):
                        n = g * PAIRS + p
                        maxima(n, p)
                        if p:
                            pt_lo(n - 1)
                        reciprocals(n, p, 0)
                        if p + 1 < PAIRS:
                            qk_lo(n + 1, p + 1)
                        reciprocals(n, p, 1)
                        if p:
                            a_lo(n - 1, p - 1)
                        if more and p == 1:
                            dve.wait_ge(s["xg_in"], 16 * (g + 2))
                            statistics(lambda t: xg[:, t, :], 2 * g + 1)
                        if more and p == 4:
                            dve.wait_ge(s["xbo"], g + 2)
                            normalize(lambda t: xg[:, t, :], "ln1", 2 * g + 1, lambda t: xg[:, t, :])
                    n = (g + 1) * PAIRS
                    if more:
                        transposed(g + 1)
                    pt_lo(n - 1)
                    a_lo(n - 1, PAIRS - 1)
                    if more:
                        values_lo(g + 1)
                        qk_lo(n, 0)
                        add_mask(g + 1)
                    for h in range(2):
                        dve.wait_ge(s["wo_d"], 1 + g * 2 + h + 1)
                        if h == 0:
                            dve.wait_ge(s["x2_kept"], 1 + g)
                            dve.wait_ge(s["xbo"], g + 1)
                        xa = xall[:, bass.ds(g * GT + 2 * h, 2), :]
                        nc.vector.tensor_tensor(x2g[:, 2 * h:2 * h + 2, :], bank_s[h][:, :].rearrange("p (t c) -> p t c", t=2), xa,
                                                ALU.add).then_inc(s["x2"], 1)
                    dve.wait_ge(s["x2"], 1 + g * 2 + 2)
                    stat = 2 * g + (2 if more else 1)
                    statistics(lambda t: x2g[:, t, :], stat)
                    normalize(lambda t: x2g[:, t, :], "ln2", stat,
                              lambda t: xrows[:, bass.ds(g * GT + t, 1), 0:C].rearrange("p a c -> p (a c)"))
                with dve.Fori(0, G - 1) as g:
                    body(g, True)
                body(G - 1, False)

            @block.tensor
            def _(pe):
                count_from_one(pe, "sc pv wo_d tp")

                def transposed(g):
                    pe.wait_ge(s["ln1"], g + 1)
                    pe.wait_ge(s["q_lo_s"], 1 + g * PAIRS)
                    pe.wait_ge(s["k_lo_s"], 1 + 2 * g * PAIRS)
                    for k in range(KC):
                        for t in range(GT):
                            last = nc.tensor.transpose((bank_q, bank_k)[k][:, t * P:(t + 1) * P], xg[:, t, k * P:(k + 1) * P], ident[:, :])
                        last.then_inc(s["xt"], 1)
                    pe.wait_ge(s["ctx_in"], 16 * (g + 1))
                    for k in range(KC):
                        for b in range(GB):
                            o = (k * GB + b) * SK
                            last = nc.tensor.transpose(bank_m[:, o:o + SK], ctxb[:, b, k * P:(k + 1) * P], ident[0:SK, 0:SK])
                    last.then_inc(s["ct"], 1)

                def project_values(g):
                    pe.wait_ge(s["ct_lo"], g + 1)
                    pe.wait_ge(s["w_lo"], 1)
                    for j in range(2 * GB):
                        b, h = j // 2, j % 2
                        if j < 2:
                            pe.wait_ge(s["p_lo"], 1 + g * PAIRS * GB)
                        if j == 3:
                            pe.wait_ge(s["a_lo"], 1 + g * PAIRS)
                        for k in range(KC):
                            last = three(pe, v_banks[j][0:SK, :],
                                         lambda lo: (cT_lo if lo else cT_hi)[:, k, b * SK:(b + 1) * SK],
                                         lambda lo: w_of(0, lo)[:, k, h * 512:(h + 1) * 512], k == 0, k == KC - 1)
                        last.then_inc(s["vp"], 1)

                def qk(n, p, xt):
                    pe.wait_ge(s["q_lo_s"], 1 + n)
                    pe.wait_ge(s["xt_lo"], xt)
                    pe.wait_ge(s["w_lo"], 3)
                    for k in range(KC):
                        last = three(pe, bank_q[:, :], lambda lo: w_of(2, lo)[:, k, p * P:(p + 1) * P],
                                     lambda lo: (xT_lo if lo else xT_hi)[:, k, :], k == 0, k == KC - 1)
                    last.then_inc(s["qk_q"], 1)
                    pe.wait_ge(s["k_lo_s"], 1 + 2 * n)
                    for k in range(KC):
                        last = three(pe, bank_k[:, 0:GB * SK], lambda lo: w_of(1, lo)[:, k, p * P:(p + 1) * P],
                                     lambda lo: (cT_lo if lo else cT_hi)[:, k, :], k == 0, k == KC - 1)
                    last.then_inc(s["qk_k"], 1)

                def scores(g, n, p):
                    pe.wait_ge(s["q_lo_s"], 1 + n + 1)
                    pe.wait_ge(s["k_lo_s"], 1 + 2 * (n + 1))
                    if p == 0:
                        pe.wait_ge(s["mb"], g + 1)
                        pe.wait_ge(s["x2"], 1 + g * 2)
                    for b in range(GB):
                        pe.wait_ge(s["ex"], 1 + ((n - 1) * GB + b + 1 if p else n * GB))
                        for t in range(QT):
                            o = bank_s[b][:, t * SK2:(t + 1) * SK2]
                            q = slice((b * QT + t) * P, (b * QT + t + 1) * P)
                            three(pe, o, lambda lo: (q_lo if lo else q_hi)[:, q],
                                  lambda lo: (k_lo if lo else k_hi)[:, b, :], True, False)
                            last = nc.tensor.matmul(o, identb[:, :], maskb[:, b * QT + t, :, :], start=False, stop=True)
                        last.then_inc(s["sc"], 1)

                def transposes(g, n, p):
                    for b in range(GB):
                        pe.wait_ge(s["nrm"], n * GB + b + 1)
                        if p:
                            pe.wait_ge(s["p_lo"], 1 + (n - 1) * GB + b + 1)
                        else:
                            pe.wait_ge(s["v_lo_s"], g * 2 * GB + 2)
                        for h in range(2):
                            for t in range(QT):
                                o = (h * QT + t) * P
                                last = nc.tensor.transpose(bank_t[b][0:SK, o:o + P], pr[:, p % 2, b * QT + t, h, :], ident[:, :])
                        last.then_inc(s["tp"], 1)

                def attend(g, n, p):
                    pe.wait_ge(s["a_lo"], 1 + n)
                    if p == 0:
                        pe.wait_ge(s["v_lo_s"], (g + 1) * 2 * GB)
                    for b in range(GB):
                        pe.wait_ge(s["p_lo"], 1 + n * GB + b + 1)
                        o = bank_o[:, b * S:(b + 1) * S]
                        for h in range(2):
                            last = three(pe, o, lambda lo: (v_lo if lo else v_hi)[:, b, p, h * D:h * D + P],
                                         lambda lo: (pT_lo if lo else pT_hi)[:, b, h, :, :], h == 0, h == 1)
                    last.then_inc(s["pv"], 1)

                pe.wait_ge(s["const"], 2)
                transposed(0)
                project_values(0)
                qk(0, 0, KC)

                def body(g, more):
                    for p in range(PAIRS):
                        n = g * PAIRS + p
                        scores(g, n, p)
                        if p:
                            transposes(g, n - 1, p - 1)
                        if p + 1 < PAIRS:
                            qk(n + 1, p + 1, (g + 1) * KC)
                        if p:
                            attend(g, n - 1, p - 1)
                    n = (g + 1) * PAIRS
                    if more:
                        transposed(g + 1)
                    transposes(g, n - 1, PAIRS - 1)
                    attend(g, n - 1, PAIRS - 1)
                    if more:
                        project_values(g + 1)
                        qk(n, 0, (g + 2) * KC)
                    pe.wait_ge(s["a_lo"], 1 + n)
                    pe.wait_ge(s["w_lo"], 4)
                    for h in range(2):
                        for t in range(2):
                            for p in range(PAIRS):
                                q = slice((2 * h + t) * P, (2 * h + t + 1) * P)
                                last = three(pe, bank_s[h][:, t * C:(t + 1) * C], lambda lo: (aT_lo if lo else aT_hi)[:, p, q],
                                             lambda lo: w_of(3, lo)[:, p, :], p == 0, p == PAIRS - 1)
                        last.then_inc(s["wo_d"], 1)
                with pe.Fori(0, G - 1) as g:
                    body(g, True)
                body(G - 1, False)

        NF = F // P
        TE = TILES * NE
        out_f = out.rearrange("b s c -> (b s) c")
        out_v = out.rearrange("b (t p) c -> p (b t) c", p=P)
        r = ExitStack()
        zT_hi = sb("zT_hi", [P, KC, TILES * P], F32R, r)
        zT_lo = sb("zT_lo", [P, KC, TILES * P], F32R, r)
        sh = sb("sh", [P, 2, GW], F32, r)
        hT_hi = sb("hT_hi", [P, NF, GW], F32R, r)
        hT_lo = sb("hT_lo", [P, NF, GW], F32R, r)
        wg_raw = sb("wg_raw", [P, KC, NE], F32, r)
        wg_hi = sb("wg_hi", [P, KC, NE], F32R, r)
        wg_lo = sb("wg_lo", [P, KC, NE], F32R, r)
        bs1c = sb("bs1c", [P, NF], F32, r)
        bs2_bc = sb("bs2_bc", [P, C], F32, r)
        rt = {n: sb("rt_" + n, [P, TILES, NE], F32, r) for n in ("d", "p", "eq", "oh1", "oh2", "p2", "tmp")}
        rm = {n: sb("rm_" + n, [P, TILES], F32, r) for n in ("m", "sum", "rs", "m1", "t1", "m2", "t2", "den", "rden", "w1", "w2", "p1", "p2")}
        assign = sb("assign", [P, NE, TILES], BF16, r)
        inc = sb("inc", [P, NE, TILES], F32, r)
        pos = sb("pos", [P, NE, TILES], F32, r)
        reset = sb("reset", [P, NE, TILES], F32, r)
        below = sb("below", [P, P], BF16, r)
        onesb = sb("onesb", [P, P], BF16, r)
        iotas = sb("iotas", [P, NE + TILES + NBLK], I32, r)
        falling = sb("falling", [P, NE], F32, r)
        blockno = sb("blockno", [P, NBLK], F32, r)
        cnt = sb("cnt", [P, NE], F32, r)
        cnti = sb("cnti", [P, NE], I32, r)
        blocks = sb("blocks", [P, NE], F32, r)
        ones8 = sb("ones8", [P, NE], F32, r)
        ends = sb("ends", [P, NE], F32, r)
        starts = sb("starts", [P, NE], F32, r)
        cmpb = sb("cmpb", [P, NBLK, NE - 1], F32, r)
        ebf = sb("ebf", [P, NBLK], F32, r)
        place = sb("place", [P, 2, TILES], I32, r)
        r.close()

        s.update({n: sem(n) for n in """zt_in ztp z_hi z_lo wgin wsh_hi wsh_lo lgt rexp rdve rpre rios
                  wsin bsin xb2 hp silu h_hi h_lo yp ysum outst scat iot rowsready placed routed""".split()})
        ws_in = [sem(f"ws_in{i}") for i in range(2)]
        ws_views = [ws1.rearrange("(k p) n -> p k n", p=P), ws2.rearrange("(k p) n -> p k n", p=P)]
        at_assign = []
        zbanks = [bank_q, bank_k, bank_m, bank_o]

        with nc.Block() as block:
            @block.sync
            def _(sp):
                for i in range(2):
                    k = ws_views[i].shape[1]
                    sp.dma_start(stage[:, i, :].rearrange("p (k n) -> p k n", k=k), ws_views[i]).then_inc(ws_in[i], 16)
                with sp.Fori(0, G) as g:
                    sp.wait_ge(s["ysum"], 1 + 2 * g + 2)
                    sp.dma_start(out_v[:, bass.ds(g * GT, GT), :], xall[:, bass.ds(g * GT, GT), :]).then_inc(s["outst"], 16)
                sp.wait_ge(s["outst"], 16 * G)

            @block.gpsimd
            def _(pool):
                nc.gpsimd.iota(iotas[:, 0:NE], pattern=[[-1, NE]], base=NE, channel_multiplier=0).then_inc(s["iot"], 1)
                nc.gpsimd.iota(iotas[:, NE:NE + TILES], pattern=[[P, TILES]], base=0, channel_multiplier=1).then_inc(s["iot"], 1)
                nc.gpsimd.iota(iotas[:, NE + TILES:], pattern=[[1, NBLK]], base=0, channel_multiplier=0).then_inc(s["iot"], 1)
                nc.gpsimd.memset(onesb[:, :], 1.0).then_inc(s["iot"], 1)
                nc.gpsimd.memset(ones8[:, :], 1.0).then_inc(s["iot"], 1)
                nc.gpsimd.memset(reset[:, :, :], 1.0).then_inc(s["iot"], 1)
                pool.wait_ge(s["iot"], 6)
                nc.gpsimd.affine_select(out=below[:, :], in_=onesb[:, :], compare_op=ALU.is_gt, fill=0.0, base=0,
                                        pattern=[[1, P]], channel_multiplier=-1).then_inc(s["iot"], 1)
                nc.gpsimd.memset(reset[:, :, 0:1], 0.0).then_inc(s["iot"], 1)
                for i in range(2):
                    pool.wait_ge(s["wsh_hi"], i + 1)
                    nc.gpsimd.tensor_tensor(wt_lo[:, i, :], stage[:, i, :], wt_hi[:, i, :].bitcast(F32),
                                            ALU.subtract).then_inc(s["wsh_lo"], 1)
                pool.wait_ge(s["placed"], 1)
                for t in range(TILES):
                    for c in range(2):
                        nc.gpsimd.indirect_dma_start(
                            out=slots, out_offset=bass.IndirectOffsetOnAxis(ap=place[:, c, t:t + 1].bitcast(U32), axis=0),
                            in_=xrows[:, t, :], in_offset=None).then_inc(s["scat"], 16)
                pool.wait_ge(s["scat"], 2 * TILES * 16)

            @block.scalar
            def _(act):
                count_from_one(act, "silu")
                act.dma_start(wg_raw[:, :, :], wg.rearrange("(k p) n -> p k n", p=P)).then_inc(s["wgin"], 16)
                act.dma_start(bs1c[:, :], bs1.rearrange("(a p) -> p a", p=P), allow_slow_non_contiguous=True).then_inc(s["bsin"], 16)
                act.dma_start(bs2_bc[:, :], bs2.rearrange("(a n) -> a n", a=1).broadcast_to([P, C])).then_inc(s["bsin"], 16)
                act.wait_ge(s["wgin"], 16)
                nc.scalar.activation(wg_hi[:, :, :], wg_raw[:, :, :], ACT.Copy).then_inc(s["wgin"], 1)
                for j in range(G * KC):
                    act.wait_ge(s["ztp"], j + 1)
                    nc.scalar.activation(zT_hi[:, j % KC, (j // KC) * GW:(j // KC + 1) * GW], zbanks[j % 4][:, :], ACT.Copy).then_inc(s["z_hi"], 1)
                for i in range(2):
                    act.wait_ge(ws_in[i], 16)
                    nc.scalar.activation(wt_hi[:, i, :], stage[:, i, :], ACT.Copy).then_inc(s["wsh_hi"], 1)
                act.wait_ge(s["rdve"], 2)
                nc.scalar.activation(rt["p"][:, :, :], rt["d"][:, :, :], ACT.Exp).then_inc(s["rexp"], 1)
                act.wait_ge(s["bsin"], 32)
                with act.Fori(0, G) as g:
                    for f in range(NF):
                        n = g * NF + f
                        act.wait_ge(s["hp"], n + 1)
                        act.wait_ge(s["h_lo"], 1 + (n - 1 if f else g * NF))
                        nc.scalar.activation(sh[:, f % 2, :], bank_s[f % 2][:, :], ACT.Silu, bias=bs1c[:, f:f + 1]).then_inc(s["silu"], 1)
                        act.wait_ge(s["silu"], 1 + n + 1)
                        if f == 0:
                            act.wait_ge(s["yp"], 1 + 2 * g)
                        nc.scalar.activation(hT_hi[:, f, :], sh[:, f % 2, :], ACT.Copy).then_inc(s["h_hi"], 1)

            @block.vector
            def _(dve):
                count_from_one(dve, "h_lo ysum")
                steps = [0]

                def link(ins):
                    steps[0] += 1
                    ins.then_inc(s["rdve"], 1)
                    dve.wait_ge(s["rdve"], steps[0])

                def over(v, n):
                    return v.rearrange("p (t a) -> p t a", a=1).broadcast_to([P, v.shape[1], n])

                dve.wait_ge(s["wgin"], 17)
                nc.vector.tensor_tensor(wg_lo[:, :, :], wg_raw[:, :, :], wg_hi[:, :, :].bitcast(F32), ALU.subtract).then_inc(s["wgin"], 1)
                for j in range(G * KC):
                    dve.wait_ge(s["z_hi"], j + 1)
                    c = slice((j // KC) * GW, (j // KC + 1) * GW)
                    nc.vector.tensor_tensor(zT_lo[:, j % KC, c], zbanks[j % 4][:, :], zT_hi[:, j % KC, c].bitcast(F32), ALU.subtract).then_inc(s["z_lo"], 1)
                lg = bank_t[0][:, 0:TE].rearrange("p (t e) -> p t e", e=NE)
                dve.wait_ge(s["lgt"], 1)
                link(nc.vector.tensor_reduce(rm["m"][:, :], lg, AX.X, ALU.max))
                link(nc.vector.tensor_tensor(rt["d"][:, :, :], lg, over(rm["m"][:, :], NE), ALU.subtract))
                dve.wait_ge(s["rexp"], 1)
                link(nc.vector.tensor_reduce(rm["sum"][:, :], rt["p"][:, :, :], AX.X, ALU.add))
                link(nc.vector.reciprocal(rm["rs"][:, :], rm["sum"][:, :]))
                link(nc.vector.tensor_tensor(rt["p"][:, :, :], rt["p"][:, :, :], over(rm["rs"][:, :], NE), ALU.mult))
                dve.wait_ge(s["iot"], 8)
                link(nc.vector.tensor_copy(falling[:, :], iotas[:, 0:NE]))
                link(nc.vector.tensor_copy(xrows[:, :, C].bitcast(I32), iotas[:, NE:NE + TILES]))
                link(nc.vector.tensor_copy(blockno[:, :], iotas[:, NE + TILES:]))
                fall = falling[:, :].rearrange("p (a e) -> p a e", a=1).broadcast_to([P, TILES, NE])

                def pick(prob, m, t, oh):
                    link(nc.vector.tensor_reduce(m, prob, AX.X, ALU.max))
                    link(nc.vector.tensor_tensor(rt["eq"][:, :, :], prob, over(m, NE), ALU.is_equal))
                    link(nc.vector.tensor_tensor(rt["eq"][:, :, :], rt["eq"][:, :, :], fall, ALU.mult))
                    link(nc.vector.tensor_reduce(t, rt["eq"][:, :, :], AX.X, ALU.max))
                    link(nc.vector.tensor_tensor(oh, fall, over(t, NE), ALU.is_equal))
                pick(rt["p"][:, :, :], rm["m1"][:, :], rm["t1"][:, :], rt["oh1"][:, :, :])
                link(nc.vector.scalar_tensor_tensor(out=rt["p2"][:, :, :], in0=rt["oh1"][:, :, :], scalar=-2.0,
                                                    in1=rt["p"][:, :, :], op0=ALU.mult, op1=ALU.add))
                pick(rt["p2"][:, :, :], rm["m2"][:, :], rm["t2"][:, :], rt["oh2"][:, :, :])
                link(nc.vector.tensor_tensor(assign[:, :, :].rearrange("p e t -> p t e"), rt["oh1"][:, :, :], rt["oh2"][:, :, :], ALU.add))
                at_assign.append(steps[0])
                link(nc.vector.scalar_tensor_tensor(out=rm["den"][:, :], in0=rm["m1"][:, :], scalar=1e-9,
                                                    in1=rm["m2"][:, :], op0=ALU.add, op1=ALU.add))
                link(nc.vector.reciprocal(rm["rden"][:, :], rm["den"][:, :]))
                link(nc.vector.tensor_tensor(rm["w1"][:, :], rm["m1"][:, :], rm["rden"][:, :], ALU.mult))
                link(nc.vector.tensor_tensor(rm["w2"][:, :], rm["m2"][:, :], rm["rden"][:, :], ALU.mult))
                link(nc.vector.tensor_tensor(rt["eq"][:, :, :], rt["oh1"][:, :, :], over(rm["w1"][:, :], NE), ALU.mult))
                link(nc.vector.tensor_tensor(rt["tmp"][:, :, :], rt["oh2"][:, :, :], over(rm["w2"][:, :], NE), ALU.mult))
                link(nc.vector.tensor_tensor(xrows[:, :, C + 1:C + 1 + NE], rt["eq"][:, :, :], rt["tmp"][:, :, :], ALU.add))
                dve.wait_ge(s["rpre"], 1)
                pre = bank_t[1][:, 0:TE].rearrange("p (e t) -> p e t", t=TILES)
                tot = bank_t[1][:, TE:2 * TE].rearrange("p (e t) -> p e t", t=TILES)
                flat1 = lambda v: v.rearrange("p e t -> p (e t)")
                link(nc.vector.tensor_tensor_scan(flat1(inc[:, :, :]), flat1(reset[:, :, :]), bank_t[1][:, TE:2 * TE], 0.0, ALU.mult, ALU.add))
                link(nc.vector.tensor_scalar(cnti[:, :], inc[:, :, TILES - 1], float(P - 1), None, ALU.add))
                link(nc.vector.tensor_scalar(cnti[:, :], cnti[:, :], 7, None, ALU.arith_shift_right))
                link(nc.vector.tensor_copy(blocks[:, :], cnti[:, :]))
                link(nc.vector.tensor_tensor_scan(ends[:, :], ones8[:, :], blocks[:, :], 0.0, ALU.mult, ALU.add))
                link(nc.vector.tensor_tensor(starts[:, :], ends[:, :], blocks[:, :], ALU.subtract))
                link(nc.vector.tensor_tensor(pos[:, :, :], inc[:, :, :], tot, ALU.subtract))
                link(nc.vector.tensor_tensor(pos[:, :, :], pos[:, :, :], pre, ALU.add))
                link(nc.vector.scalar_tensor_tensor(out=pos[:, :, :], in0=over(starts[:, :], TILES), scalar=float(P),
                                                    in1=pos[:, :, :], op0=ALU.mult, op1=ALU.add))
                for c in range(2):
                    link(nc.vector.tensor_tensor(rt["tmp"][:, :, :], rt[("oh1", "oh2")[c]][:, :, :],
                                                 pos[:, :, :].rearrange("p e t -> p t e"), ALU.mult))
                    link(nc.vector.tensor_reduce(rm[("p1", "p2")[c]][:, :], rt["tmp"][:, :, :], AX.X, ALU.add))
                    link(nc.vector.tensor_copy(place[:, c, :], rm[("p1", "p2")[c]][:, :]))
                nc.vector.tensor_copy(startsi[:, :], starts[:, :]).then_inc(s["placed"], 1)
                link(nc.vector.tensor_tensor(cmpb[:, :, :], over(blockno[:, :], NE - 1),
                                             starts[:, 1:NE].rearrange("p (a e) -> p a e", a=1).broadcast_to([P, NBLK, NE - 1]), ALU.is_ge))
                link(nc.vector.tensor_reduce(ebf[:, :], cmpb[:, :, :], AX.X, ALU.add))
                link(nc.vector.tensor_copy(ebi[:, 0, :], ebf[:, :]))
                link(nc.vector.tensor_scalar(ebi[:, 1, :], ebi[:, 0, :], 1, None, ALU.bitwise_and))
                dve.wait_ge(s["bsin"], 32)
                nc.vector.tensor_scalar(bs2_bc[:, :], bs2_bc[:, :], SHARED, None, ALU.mult).then_inc(s["xb2"], 1)
                dve.wait_ge(s["xb2"], 1)
                for g in range(G):
                    nc.vector.tensor_tensor(xall[:, g * GT:(g + 1) * GT, :], xall[:, g * GT:(g + 1) * GT, :],
                                            bs2_bc[:, :].rearrange("p (a c) -> p a c", a=1).broadcast_to([P, GT, C]),
                                            ALU.add).then_inc(s["xb2"], 1)
                dve.wait_ge(s["xb2"], 1 + G)
                with dve.Fori(0, G) as g:
                    for f in range(NF):
                        dve.wait_ge(s["h_hi"], g * NF + f + 1)
                        nc.vector.tensor_tensor(hT_lo[:, f, :], sh[:, f % 2, :], hT_hi[:, f, :].bitcast(F32), ALU.subtract).then_inc(s["h_lo"], 1)
                    for h in range(2):
                        dve.wait_ge(s["yp"], 1 + 2 * g + h + 1)
                        xa = xall[:, bass.ds(g * GT + 2 * h, 2), :].rearrange("p t c -> p (t c)")
                        nc.vector.scalar_tensor_tensor(out=xa, in0=(bank_m, bank_o)[h][:, :], scalar=SHARED, in1=xa,
                                                       op0=ALU.mult, op1=ALU.add).then_inc(s["ysum"], 1)

            @block.tensor
            def _(pe):
                count_from_one(pe, "yp")
                for j in range(G * KC):
                    k, c = j % KC, j // KC
                    if j >= 4:
                        pe.wait_ge(s["z_lo"], j - 3)
                    for t in range(GT):
                        last = nc.tensor.transpose(zbanks[j % 4][:, t * P:(t + 1) * P], xrows[:, c * GT + t, k * P:(k + 1) * P], ident[:, :])
                    last.then_inc(s["ztp"], 1)
                pe.wait_ge(s["z_lo"], G * KC)
                pe.wait_ge(s["wgin"], 18)
                for t in range(TILES):
                    for k in range(KC):
                        last = three(pe, bank_t[0][:, t * NE:(t + 1) * NE], lambda lo: (zT_lo if lo else zT_hi)[:, k, t * P:(t + 1) * P],
                                     lambda lo: (wg_lo if lo else wg_hi)[:, k, :], k == 0, k == KC - 1)
                last.then_inc(s["lgt"], 1)

                def prefix():
                    pe.wait_ge(s["iot"], 8)
                    pe.wait_ge(s["rdve"], at_assign[0])
                    a = assign[:, :, :].rearrange("p e t -> p (e t)")
                    nc.tensor.matmul(bank_t[1][:, 0:TE], below[:, :], a, start=True, stop=True)
                    nc.tensor.matmul(bank_t[1][:, TE:2 * TE], onesb[:, :], a, start=True, stop=True).then_inc(s["rpre"], 1)
                prefix()
                pe.wait_ge(s["wsh_lo"], 2)
                with pe.Fori(0, G) as g:
                    for f in range(NF):
                        n = g * NF + f
                        pe.wait_ge(s["silu"], 1 + (n - 1 if f else g * NF))
                        for k in range(KC):
                            last = three(pe, bank_s[f % 2][:, :], lambda lo: w_of(0, lo, ws_views[0])[:, k, f * P:(f + 1) * P],
                                         lambda lo: (zT_lo if lo else zT_hi)[:, k, bass.ds(g * GW, GW)], k == 0, k == KC - 1)
                        last.then_inc(s["hp"], 1)
                    pe.wait_ge(s["h_lo"], 1 + (g + 1) * NF)
                    for h in range(2):
                        pe.wait_ge(s["ysum"], 1 + 2 * g)
                        for t in range(2):
                            for f in range(NF):
                                q = slice((2 * h + t) * P, (2 * h + t + 1) * P)
                                last = three(pe, (bank_m, bank_o)[h][:, t * C:(t + 1) * C], lambda lo: (hT_lo if lo else hT_hi)[:, f, q],
                                             lambda lo: w_of(1, lo, ws_views[1])[:, f, :], f == 0, f == NF - 1)
                        last.then_inc(s["yp"], 1)

        U = 4
        e_ = ExitStack()
        we1 = sb("we1", [P, 2, KC, F], F32, e_)
        we2 = sb("we2", [P, 2, NF, C], F32, e_)
        b1_bc = sb("b1_bc", [P, 2, F], F32, e_)
        b2_bc = sb("b2_bc", [P, NE, C], F32, e_)
        xs = sb("xs", [P, U, ROW], F32, e_)
        xsT = sb("xsT", [P, 2, KC, P], F32, e_)
        hb = sb("hb", [P, 2, F], F32, e_)
        hbT = sb("hbT", [P, NF, P], F32, e_)
        yb = sb("yb", [P, 2, C], F32, e_)
        nop = sb("nop", [P, 1], F32, e_)
        nop_to = sb("nop_to", [P, 1], F32, e_)
        yw = sb("yw", [P, 2, C], F32, e_)
        e_.close()
        s.update({n: sem(n) for n in "b2in we_in we_ready xsT_p xsT_c g1 hbias hsilu hT_p hTc_act hTc_dve g2 yadd yw_s added nopped".split()})
        xs_in = [sem(f"xs_in{i}") for i in range(U)]
        bank_h, bank_x, bank_y, bank_hT = bank_s, bank_q, bank_m, bank_t
        LOOP = (NBLK - 3) // U

        def steps(eng, step):
            with eng.Fori(0, LOOP) as j:
                for u in range(U):
                    step(U * j + u, u, U, j)
            for i in range(U * LOOP, NBLK):
                step(i, i % U, NBLK - 1 - i, i // U)

        with nc.Block() as block:
            @block.sync
            def _(sp):
                sp.dma_start(b2_bc[:, :, :], b2.rearrange("(a e) c -> a e c", a=1).broadcast_to([P, NE, C])).then_inc(s["b2in"], 16)
                for e in range(NE):
                    if e >= 2:
                        sp.wait_ge(s["g2"], 1 + sp.value_load(startsi[0:1, e - 1:e], min_val=0, max_val=NBLK))
                    sp.dma_start(we1[:, e % 2, :, :], w1[e].rearrange("(k p) n -> p k n", p=P)).then_inc(s["we_in"], 16)
                    sp.dma_start(we2[:, e % 2, :, :], w2[e].rearrange("(k p) n -> p k n", p=P)).then_inc(s["we_in"], 16)
                    sp.dma_start(b1_bc[:, e % 2, :], b1[e:e + 1, :].broadcast_to([P, F])).then_inc(s["we_in"], 16)
                    sp.wait_ge(s["we_in"], 48 * (e + 1))
                    sp.sem_inc(s["we_ready"], 1)

            @block.gpsimd
            def _(pool):
                nc.gpsimd.memset(nop[:, :], 0.0).then_inc(s["nopped"], 1)
                pool.wait_ge(s["nopped"], 1)
                pool.dma_start(nop_to[:, :], nop[:, :]).then_inc(s["added"], 16)
                last_token = pool.to_reg(B * S - 1)

                def step(i, u, left, turn):
                    pool.wait_ge(s["yw_s"], i + 1)
                    pool.wait_ge(s["added"], 16 * (i + 1))
                    pool.wait_ge(s["nopped"], i + 1)
                    nc.gpsimd.tensor_tensor(nop[:, :], nop[:, :], nop[:, :], ALU.add).then_inc(s["nopped"], 1)
                    nc.gpsimd.indirect_dma_start(
                        out=out_f, out_offset=bass.IndirectOffsetOnAxis(ap=xs[:, u, C:C + 1].bitcast(U32), axis=0),
                        in_=yw[:, u % 2, :], in_offset=None, bounds_check=last_token, oob_is_err=False,
                        compute_op=ALU.add).then_inc(s["added"], 16)
                steps(pool, step)
                pool.wait_ge(s["added"], 16 * (NBLK + 1))

            @block.scalar
            def _(act):
                count_from_one(act, "hTc_act")
                def load(i, u):
                    act.dma_start(xs[:, u, :], slots[bass.ds(i * P, P), :]).then_inc(xs_in[u], 16)

                def silu(i, u):
                    for h in range(2):
                        act.wait_ge(s["hbias"], 2 * i + h + 1)
                        hv = hb[:, u % 2, h * 512:(h + 1) * 512]
                        nc.scalar.activation(hv, hv, ACT.Silu).then_inc(s["hsilu"], 1)

                def rows_t(i, u):
                    act.wait_ge(s["xsT_p"], i + 1)
                    nc.scalar.activation(xsT[:, u % 2, :, :], bank_x[:, 0:KC * P], ACT.Copy).then_inc(s["xsT_c"], 1)

                def step(i, u, left, turn):
                    act.wait_ge(s["hT_p"], 2 * i + 1)
                    nc.scalar.activation(hbT[:, 0:NF // 2, :], bank_hT[0][:, :], ACT.Copy).then_inc(s["hTc_act"], 1)
                    if left >= 1:
                        silu(i + 1, u + 1)
                    if left >= 2:
                        rows_t(i + 2, u + 2)
                    if left >= 3:
                        act.wait_ge(s["added"], 16 * (i + 1))
                        load(i + 3, (u + 3) % U)
                for i in range(3):
                    load(i, i)
                rows_t(0, 0)
                silu(0, 0)
                rows_t(1, 1)
                steps(act, step)

            @block.vector
            def _(dve):
                count_from_one(dve, "hTc_dve yadd")
                def bias(i, u):
                    slot = dve.value_load(ebi[0:1, 1, bass.ds(i, 1)], min_val=0, max_val=1)
                    for h in range(2):
                        dve.wait_ge(s["g1"], 2 * i + h + 1)
                        nc.vector.tensor_tensor(hb[:, u % 2, h * 512:(h + 1) * 512], bank_h[h][:, :],
                                                b1_bc[:, bass.ds(slot, 1), h * 512:(h + 1) * 512].rearrange("p a n -> p (a n)"),
                                                ALU.add).then_inc(s["hbias"], 1)

                def step(i, u, left, turn):
                    dve.wait_ge(s["hT_p"], 2 * i + 2)
                    nc.vector.tensor_copy(hbT[:, NF // 2:, :].rearrange("p f q -> p (f q)"), bank_hT[1][:, :]).then_inc(s["hTc_dve"], 1)
                    if left >= 1:
                        bias(i + 1, u + 1)
                    e = dve.value_load(ebi[0:1, 0, bass.ds(i, 1)], min_val=0, max_val=NE - 1)
                    dve.wait_ge(s["g2"], 1 + i + 1)
                    nc.vector.tensor_tensor(yb[:, u % 2, :], bank_y[:, 0:C], b2_bc[:, bass.ds(e, 1), :].rearrange("p a c -> p (a c)"),
                                            ALU.add).then_inc(s["yadd"], 1)
                    dve.wait_ge(s["added"], 16 * (i + 1))
                    dve.wait_ge(s["yadd"], 1 + i + 1)
                    nc.vector.tensor_scalar(yw[:, u % 2, :], yb[:, u % 2, :], xs[:, u, bass.ds(e + (C + 1), 1)], None,
                                            ALU.mult).then_inc(s["yw_s"], 1)
                dve.wait_ge(s["b2in"], 16)
                bias(0, 0)
                steps(dve, step)

            @block.tensor
            def _(pe):
                count_from_one(pe, "g2")
                def rows_t(i, u, at):
                    pe.wait_ge(xs_in[u], 16 * (at + 1))
                    pe.wait_ge(s["xsT_c"], i)
                    for k in range(KC):
                        last = nc.tensor.transpose(bank_x[:, k * P:(k + 1) * P], xs[:, u, k * P:(k + 1) * P], ident[:, :])
                    last.then_inc(s["xsT_p"], 1)

                def up(i, u):
                    e = pe.value_load(ebi[0:1, 0, bass.ds(i, 1)], min_val=0, max_val=NE - 1)
                    slot = pe.value_load(ebi[0:1, 1, bass.ds(i, 1)], min_val=0, max_val=1)
                    pe.wait_ge(s["we_ready"], e + 1)
                    pe.wait_ge(s["xsT_c"], i + 1)
                    for h in range(2):
                        pe.wait_ge(s["hbias"], 2 * i)
                        for k in range(KC):
                            last = nc.tensor.matmul(bank_h[h][:, :], xsT[:, u % 2, k, :],
                                                    we1[:, bass.ds(slot, 1), k, h * 512:(h + 1) * 512].rearrange("p a n -> p (a n)"),
                                                    start=k == 0, stop=k == KC - 1)
                        last.then_inc(s["g1"], 1)

                def step(i, u, left, turn):
                    pe.wait_ge(s["hTc_act"], 1 + i)
                    pe.wait_ge(s["hTc_dve"], 1 + i)
                    for h in range(2):
                        pe.wait_ge(s["hsilu"], 2 * i + h + 1)
                        for f in range(NF // 2):
                            o = (h * NF // 2 + f) * P
                            last = nc.tensor.transpose(bank_hT[h][:, f * P:(f + 1) * P], hb[:, u % 2, o:o + P], ident[:, :])
                        last.then_inc(s["hT_p"], 1)
                    if left >= 1:
                        up(i + 1, u + 1)
                    if left >= 2:
                        rows_t(i + 2, (u + 2) % U, turn + (u + 2) // U)
                    slot = pe.value_load(ebi[0:1, 1, bass.ds(i, 1)], min_val=0, max_val=1)
                    pe.wait_ge(s["hTc_act"], 1 + i + 1)
                    pe.wait_ge(s["hTc_dve"], 1 + i + 1)
                    pe.wait_ge(s["yadd"], 1 + i)
                    for f in range(NF):
                        last = nc.tensor.matmul(bank_y[:, 0:C], hbT[:, f, :], we2[:, bass.ds(slot, 1), f, :].rearrange("p a c -> p (a c)"),
                                                start=f == 0, stop=f == NF - 1)
                    last.then_inc(s["g2"], 1)
                rows_t(0, 0, 0)
                up(0, 0)
                rows_t(1, 1, 0)
                steps(pe, step)


_INS = ['x', 'ctx_1024', 'mask_BxSxS2_bk1'] + ['L0_xattn_' + n for n in ('Wq', 'bq', 'Wk', 'bk', 'Wv', 'bv', 'Wo', 'bo')] \
    + ['L0_ffn_' + n for n in ('Wg', 'W1', 'b1', 'W2', 'b2', 'Ws1', 'bs1', 'Ws2', 'bs2')]


def kernel(**inputs):
    import numpy as _np
    import concourse.bacc as _bacc
    from concourse import mybir as _mybir
    from concourse.bass_utils import run_bass_kernel_spmd as _run

    nc = _bacc.Bacc("TRN2", target_bir_lowering=False, num_devices=1)
    arrays, args = {}, []
    for name in _INS:
        a = _np.ascontiguousarray(inputs[name])
        arrays[f"in_{name}"] = a
        args.append(nc.dram_tensor(f"in_{name}", a.shape, _mybir.dt.from_np(a.dtype), kind="ExternalInput").ap())
    shape = inputs['x'].shape
    out = nc.dram_tensor("out_dram", shape, _mybir.dt.float32, kind="ExternalOutput").ap()
    xattn_moe_kernel(nc, *args, out)
    r = _run(nc, [arrays], core_ids=[0])
    return r.results[0]["out_dram"]
```

```python
import concourse.bass as bass
from concourse import mybir
from contextlib import ExitStack

F32 = mybir.dt.float32
F32R = mybir.dt.float32r
BF16 = mybir.dt.bfloat16
I32 = mybir.dt.int32
U32 = mybir.dt.uint32
U8 = mybir.dt.uint8
ALU = mybir.AluOpType
ACT = mybir.ActivationFunctionType
AX = mybir.AxisListType


def xattn_moe_kernel(nc, x, ctx_in, mask, wq, bq, wk, bk, wv, bv, wo, bo,
                     wg, w1, b1, w2, b2, ws1, bs1, ws2, bs2, out):
    B, S, C = x.shape
    SK = ctx_in.shape[1]
    HD = wq.shape[1]
    D = 64
    P = 128
    KC = C // P
    PAIRS = HD // P
    TILES = B * S // P
    GB = 2
    G = B // GB
    GT = TILES // G
    QT = S // P
    GW = GT * P
    SK2 = 2 * SK
    VW = 3 * D
    EPS = 1e-5
    SHARED = 0.1
    SCALE = D ** -0.5
    NE = wg.shape[1]
    F = w1.shape[2]
    NBLK = 2 * TILES + NE - 1
    NOBODY = B * S
    ROW = C + 9
    MASKED = -1e30

    es = ExitStack()
    with es:
        def sem(name):
            return es.enter_context(nc.semaphore(name))

        def sb(name, shape, dt, stack=es):
            return stack.enter_context(nc.sbuf_tensor(name, shape, dt))

        ident = sb("ident", [P, P], F32)
        identb = sb("identb", [P, P], BF16)
        xall = sb("xall", [P, TILES, C], F32)
        xrows = sb("xrows", [P, TILES, ROW], F32)
        wt_a = sb("wt_a", [P, 2, 2, KC * HD], F32R)
        stage = sb("stage", [P, 2, KC * HD], F32)

        startsi = sb("startsi", [P, NE], I32)
        ebi = sb("ebi", [P, 2, NBLK], I32)
        slots = nc.dram_tensor("slots", (NBLK * P, ROW), F32, kind="Internal").ap()

        qo = ExitStack()
        wt_b = sb("wt_b", [P, 2, 2, KC * HD], F32R, qo)
        wt_hi = [(wt_a, wt_b)[i // 2][:, 0, i % 2, :] for i in range(4)]
        wt_lo = [(wt_a, wt_b)[i // 2][:, 1, i % 2, :] for i in range(4)]
        a = ExitStack()
        xg = sb("xg", [P, GT, C], F32, a)
        ctxb = sb("ctxb", [SK, GB, C], F32, a)
        masku = sb("masku", [P, GT, SK], U8, a)
        maskb = sb("maskb", [P, GT, 2, SK], BF16, a)
        xT_hi = sb("xT_hi", [P, KC, GW], F32R, a)
        xT_lo = sb("xT_lo", [P, KC, GW], F32R, a)
        cT_hi = sb("cT_hi", [P, KC, GB * SK], F32R, a)
        cT_lo = sb("cT_lo", [P, KC, GB * SK], F32R, a)
        v_hi = sb("v_hi", [SK, GB, PAIRS, VW], F32R, a)
        v_lo = sb("v_lo", [SK, GB, PAIRS, VW], F32R, a)
        q_hi = sb("q_hi", [P, GW], F32R, a)
        q_lo = sb("q_lo", [P, GW], F32R, a)
        k_hi = sb("k_hi", [P, GB, SK2], F32R, a)
        k_lo = sb("k_lo", [P, GB, SK2], F32R, a)
        pT_hi = sb("pT_hi", [SK, GB, 2, QT, P], F32R, a)
        pT_lo = sb("pT_lo", [SK, GB, 2, QT, P], F32R, a)
        aT_hi = sb("aT_hi", [P, PAIRS, GW], F32R, a)
        aT_lo = sb("aT_lo", [P, PAIRS, GW], F32R, a)
        bqk = sb("bqk", [P, 3, PAIRS], F32, a)
        bo_bc = sb("bo_bc", [P, C], F32, a)
        stats = sb("stats", [P, GT, 6], F32, a)
        mv = sb("mv", [P, GT, 2], F32, a)
        rstd = sb("rstd", [P, GT], F32, a)
        fence = sb("fence", [P, 1], F32, a)
        vareps = sb("vareps", [P, GT], F32, a)
        mhalf = sb("mhalf", [P, GT], F32, a)
        epst = sb("epst", [P, GT], F32, a)
        nmax = sb("nmax", [P, 2, GT, 2], F32, a)
        ssum = sb("ssum", [P, 2, GT, 2], F32, a)
        rsum = sb("rsum", [P, 2, GT, 2], F32, a)
        a.close()

        flat = stage[:, :, :].rearrange("p a n -> p (a n)")
        x2g = flat[:, 2 * GT * SK2:2 * GT * SK2 + GT * C].rearrange("p (t c) -> p t c", t=GT)
        pad_at = 2 * GT * SK2 + GT * C
        padrow = flat[:, pad_at:pad_at + ROW]
        pr = flat[:, 0:2 * GT * SK2] \
            .rearrange("p (r t h k) -> p r t h k", r=2, t=GT, h=2)

        ps = ExitStack()

        def pb(name):
            return ps.enter_context(nc.psum_tensor(name, [P, 512], F32))
        bank_q, bank_k, bank_m, bank_o = pb("bank_q"), pb("bank_k"), pb("bank_m"), pb("bank_o")
        bank_s = [pb("bank_s0"), pb("bank_s1")]
        bank_t = [pb("bank_t0"), pb("bank_t1")]
        ps.close()

        names = """wo_lo pad padded ve x2_kept bias_in bo_in bq_s xg_in mask_in ctx_in w_hi w_lo const zeros ln1 xbo xt ct
                   xt_hi xt_lo ct_hi ct_lo vp v_hi_s v_lo_s mb qk_q qk_k q_hi_s k_hi_s q_lo_s k_lo_s
                   sc mx ex rc nrm tp p_hi p_lo pv a_hi a_lo wo_d x2 ln2 dv_st dv_ag dv_rs""".split()
        s = {n: sem(n) for n in names}
        v_banks = [bank_t[0], bank_t[1], bank_m, bank_o]
        wraw_in = [sem(f"wraw_in{i}") for i in range(4)]

        x_v = x.rearrange("b (t p) c -> p (b t) c", p=P)
        m_v = mask.rearrange("b (t p) k -> p (b t) k", p=P)
        w_views = [wv.rearrange("(k p) n -> p k n", p=P), wk.rearrange("(k p) n -> p k n", p=P),
                   wq.rearrange("(k p) n -> p k n", p=P), wo.rearrange("(k p) n -> p k n", p=P)]
        ctx_v = ctx_in.rearrange("b k c -> k b c")

        def w_of(i, lo, view=None):
            return (wt_lo if lo else wt_hi)[i].rearrange("p (k n) -> p k n", n=(w_views[i] if view is None else view).shape[2])

        def count_from_one(eng, names):
            for n in names.split():
                eng.sem_inc(s[n], 1)

        def three(pe, o, st, mo, first, last):
            nc.tensor.matmul(o, st(0), mo(0), start=first, stop=False)
            nc.tensor.matmul(o, st(0), mo(1), start=False, stop=False)
            return nc.tensor.matmul(o, st(1), mo(0), start=False, stop=last)

        LN_TILES = ((0, 1), (2,), (3,))

        with nc.Block() as block:
            @block.sync
            def _(sp):
                def load_weight(i):
                    k = w_views[i].shape[1]
                    sp.dma_start(stage[:, i % 2, :].rearrange("p (k n) -> p k n", k=k), w_views[i]).then_inc(wraw_in[i], 16)
                sp.dma_start(xg[:, :, :], x_v[:, 0:GT, :]).then_inc(s["xg_in"], 16)
                sp.dma_start(ctxb[:, :, :], ctx_v[:, 0:GB, :]).then_inc(s["ctx_in"], 16)
                load_weight(0)
                load_weight(1)
                sp.dma_start(masku[:, :, :], m_v[:, 0:GT, :]).then_inc(s["mask_in"], 16)
                for i in (2, 3):
                    sp.wait_ge(s["w_lo"], i - 1)
                    load_weight(i)
                with sp.Fori(1, G) as g:
                    sp.wait_ge(s["mb"], g)
                    sp.dma_start(masku[:, :, :], m_v[:, bass.ds(g * GT, GT), :]).then_inc(s["mask_in"], 16)
                    sp.wait_ge(s["xt"], g * KC)
                    sp.dma_start(xg[:, :, :], x_v[:, bass.ds(g * GT, GT), :]).then_inc(s["xg_in"], 16)
                    sp.wait_ge(s["ct"], g)
                    sp.dma_start(ctxb[:, :, :], ctx_v[:, bass.ds(g * GB, GB), :]).then_inc(s["ctx_in"], 16)
                sp.wait_ge(s["pad"], 2)
                sp.dma_start(slots.rearrange("(b p) n -> p b n", p=P), padrow[:, :].rearrange("p (a n) -> p a n", a=1)
                             .broadcast_to([P, NBLK, ROW])).then_inc(s["padded"], 16)
                sp.wait_ge(s["padded"], 16)

            @block.gpsimd
            def _(pool):
                count_from_one(pool, "x2_kept")
                pool.dma_start(bo_bc[:, :], bo.rearrange("(a n) -> a n", a=1).broadcast_to([P, C])).then_inc(s["bo_in"], 16)

                def rsqrt(stat):
                    pool.wait_ge(s["dv_ag"], stat * GT + GT)
                    nc.gpsimd.tensor_tensor(vareps[:, :], mv[:, :, 1], epst[:, :], ALU.add).then_inc(s["ve"], 1)
                    pool.wait_ge(s["ve"], stat + 1)
                    nc.gpsimd.tensor_tensor(rstd[:, :], vareps[:, :], mhalf[:, :], ALU.pow).then_inc(s["dv_rs"], 1)

                def add_bo(g, h):
                    nc.gpsimd.tensor_tensor(xall[:, bass.ds(g * GT + 2 * h, 2), :], xg[:, 2 * h:2 * h + 2, :],
                                            bo_bc[:, :].rearrange("p (a c) -> p a c", a=1).broadcast_to([P, 2, C]),
                                            ALU.add).then_inc(s["xbo"], 1)

                def scale(n, p):
                    for b in range(GB):
                        pool.wait_ge(s["rc"], n * GB + b + 1)
                        pt = pr[:, p % 2, b * QT:(b + 1) * QT, :, :]
                        nc.gpsimd.tensor_tensor(
                            pt, pt, rsum[:, p % 2, b * QT:(b + 1) * QT, :].rearrange("p t (h a) -> p t h a", a=1)
                            .broadcast_to([P, QT, 2, SK]), ALU.mult).then_inc(s["nrm"], 1)

                nc.gpsimd.memset(mhalf[:, :], -0.5).then_inc(s["zeros"], 1)
                nc.gpsimd.memset(epst[:, :], EPS).then_inc(s["zeros"], 1)
                nc.gpsimd.memset(ident[:, :], 0.0).then_inc(s["zeros"], 1)
                nc.gpsimd.memset(identb[:, :], 0.0).then_inc(s["zeros"], 1)
                pool.wait_ge(s["zeros"], 4)
                for m in (ident, identb):
                    nc.gpsimd.affine_select(out=m[:, :], in_=m[:, :], compare_op=ALU.not_equal, fill=1.0, base=0,
                                            pattern=[[-1, P]], channel_multiplier=1).then_inc(s["const"], 1)
                pool.wait_ge(s["bo_in"], 16)
                pool.wait_ge(s["xg_in"], 16)
                add_bo(0, 0)
                rsqrt(0)
                for z in (v_hi, v_lo, k_hi, k_lo):
                    nc.gpsimd.memset(z[:].bitcast(F32), 0.0).then_inc(s["const"], 1)
                scale(0, 0)
                pool.wait_ge(s["w_hi"], 4)
                nc.gpsimd.tensor_tensor(wt_lo[3], stage[:, 1, :], wt_hi[3].bitcast(F32), ALU.subtract).then_inc(s["wo_lo"], 1)
                pool.wait_ge(s["wo_lo"], 1)
                nc.gpsimd.memset(padrow[:, :], 0.0).then_inc(s["pad"], 1)
                pool.wait_ge(s["pad"], 1)
                nc.gpsimd.memset(padrow[:, C:C + 1].bitcast(I32), NOBODY).then_inc(s["pad"], 1)

                def keep(g, h):
                    pool.wait_ge(s["x2"], 1 + g * 2 + h + 1)
                    nc.gpsimd.tensor_copy(xall[:, bass.ds(g * GT + 2 * h, 2), :], x2g[:, 2 * h:2 * h + 2, :]).then_inc(s["x2_kept"], 1)

                def body(g, more):
                    for p in range(1, PAIRS):
                        scale(g * PAIRS + p, p)
                        if more and p == 2:
                            rsqrt(2 * g + 1)
                        if more and p in (2, 3):
                            add_bo(g + 1, p - 2)
                    if more:
                        scale((g + 1) * PAIRS, 0)
                    keep(g, 0)
                    rsqrt(2 * g + (2 if more else 1))
                    keep(g, 1)
                with pool.Fori(0, G - 1) as g:
                    body(g, True)
                body(G - 1, False)

            @block.scalar
            def _(act):
                count_from_one(act, "ex")
                for i, bb in enumerate((bq, bk, bv)):
                    act.dma_start(bqk[:, i, :], bb.rearrange("(a p) -> p a", p=P), allow_slow_non_contiguous=True).then_inc(s["bias_in"], 16)

                def split_weight(i):
                    act.wait_ge(wraw_in[i], 16)
                    nc.scalar.activation(wt_hi[i], stage[:, i % 2, :], ACT.Copy, scale=SCALE if i == 2 else 1.0).then_inc(s["w_hi"], 1)

                def transposed(g):
                    for k in range(KC):
                        act.wait_ge(s["xt"], g * KC + k + 1)
                        nc.scalar.activation(xT_hi[:, k, :], (bank_q, bank_k)[k][:, :], ACT.Copy).then_inc(s["xt_hi"], 1)
                    act.wait_ge(s["ct"], g + 1)
                    nc.scalar.activation(cT_hi[:, :, :], bank_m[:, 0:KC * GB * SK], ACT.Copy).then_inc(s["ct_hi"], 1)

                def values_hi(g):
                    for j in range(2 * GB):
                        act.wait_ge(s["vp"], g * 2 * GB + j + 1)
                        b, h = j // 2, j % 2
                        vin = v_banks[j][0:SK, :].rearrange("p (a e d) -> p a e d", e=2, d=D)
                        vout = v_hi[:, b, h * PAIRS // 2:(h + 1) * PAIRS // 2, :] \
                            .rearrange("p a (e d) -> p a e d", d=D)[:, :, 0:3:2, :]
                        nc.scalar.activation(vout, vin, ACT.Copy).then_inc(s["v_hi_s"], 1)

                def qk_hi(n, p):
                    act.wait_ge(s["qk_q"], n + 1)
                    act.wait_ge(s["sc"], 1 + n * GB)
                    nc.scalar.activation(q_hi[:, :], bank_q[:, :], ACT.Identity, bias=bqk[:, 0, p:p + 1]).then_inc(s["q_hi_s"], 1)
                    act.wait_ge(s["qk_k"], n + 1)
                    for e in range(2):
                        r = slice(e * D, (e + 1) * D)
                        nc.scalar.activation(k_hi[r, :, e * SK:(e + 1) * SK],
                                             bank_k[r, 0:GB * SK].rearrange("p (b k) -> p b k", b=GB),
                                             ACT.Identity, bias=bqk[r, 1, p:p + 1]).then_inc(s["k_hi_s"], 1)

                def exps(n, p, b):
                    act.wait_ge(s["tp"], 1 + ((n - 1) * GB if p else n * GB))
                    act.wait_ge(s["mx"], n * GB + b + 1)
                    for t in range(QT):
                        for h in range(2):
                            o = (t * 2 + h) * SK
                            st = (slice(None), p % 2, b * QT + t, slice(h, h + 1))
                            last = nc.scalar.activation(pr[:, p % 2, b * QT + t, h, :], bank_s[b][:, o:o + SK], ACT.Exp,
                                                        bias=nmax[st], accum_out=ssum[st])
                    last.then_inc(s["ex"], 1)

                def pt_hi(n):
                    for b in range(GB):
                        act.wait_ge(s["tp"], 1 + n * GB + b + 1)
                        act.wait_ge(s["pv"], 1 + n)
                        nc.scalar.activation(pT_hi[:, b, :, :, :], bank_t[b][0:SK, :], ACT.Copy).then_inc(s["p_hi"], 1)

                def a_hi(g, n, p):
                    act.wait_ge(s["pv"], 1 + n + 1)
                    if p == 0:
                        act.wait_ge(s["wo_d"], 1 + g * 2)
                    nc.scalar.activation(aT_hi[:, p, :], bank_o[:, :], ACT.Identity, bias=bqk[:, 2, p:p + 1]).then_inc(s["a_hi"], 1)

                split_weight(0)
                act.wait_ge(s["const"], 4)
                transposed(0)
                split_weight(1)
                values_hi(0)
                split_weight(2)
                act.wait_ge(s["bias_in"], 48)
                act.wait_ge(s["bq_s"], 1)
                act.wait_ge(s["const"], 6)
                qk_hi(0, 0)

                def turn(g):
                    n = g * PAIRS
                    exps(n, 0, 0)
                    qk_hi(n + 1, 1)
                    exps(n, 0, 1)

                def body(g, more):
                    for p in range(1, PAIRS):
                        n = g * PAIRS + p
                        exps(n, p, 0)
                        pt_hi(n - 1)
                        if p + 1 < PAIRS:
                            qk_hi(n + 1, p + 1)
                        elif more:
                            transposed(g + 1)
                        exps(n, p, 1)
                        a_hi(g, n - 1, p - 1)
                    n = (g + 1) * PAIRS
                    if more:
                        qk_hi(n, 0)
                    pt_hi(n - 1)
                    if more:
                        turn(g + 1)
                    a_hi(g, n - 1, PAIRS - 1)
                    if more:
                        values_hi(g + 1)
                turn(0)
                split_weight(3)
                with act.Fori(0, G - 1) as g:
                    body(g, True)
                body(G - 1, False)

            @block.vector
            def _(dve):
                count_from_one(dve, "x2 p_lo a_lo q_lo_s k_lo_s")

                def sums(tile, tiles):
                    for t in tiles:
                        nc.vector.bn_stats(stats[:, t, :], tile(t)).then_inc(s["dv_st"], 1)

                def statistics(stat):
                    dve.wait_ge(s["dv_st"], stat * GT + GT)
                    nc.vector.memset(fence[:, :], 0.0)
                    for t in range(GT):
                        nc.vector.bn_aggr(mv[:, t, :], stats[:, t, :]).then_inc(s["dv_ag"], 1)

                def normalize(tile, done, stat, dst, tiles=range(GT)):
                    dve.wait_ge(s["dv_rs"], stat + 1)
                    for t in tiles:
                        last = nc.vector.tensor_scalar(dst(t), tile(t), mv[:, t, 0:1], rstd[:, t:t + 1],
                                                       ALU.subtract, ALU.mult)
                    last.then_inc(s[done], 1)

                def weight_lo(i):
                    dve.wait_ge(s["w_hi"], i + 1)
                    nc.vector.scalar_tensor_tensor(out=wt_lo[i], in0=stage[:, i % 2, :], scalar=SCALE if i == 2 else 1.0,
                                                   in1=wt_hi[i].bitcast(F32), op0=ALU.mult, op1=ALU.subtract).then_inc(s["w_lo"], 1)

                def add_mask(g):
                    dve.wait_ge(s["sc"], 1 + g * PAIRS * GB)
                    dve.wait_ge(s["mask_in"], 16 * (g + 1))
                    nc.vector.tensor_scalar(maskb[:, :, :, :], masku[:, :, :]
                                            .rearrange("p t (a k) -> p t a k", a=1).broadcast_to([P, GT, 2, SK]),
                                            MASKED, None, ALU.mult).then_inc(s["mb"], 1)

                def transposed(g):
                    for k in range(KC):
                        dve.wait_ge(s["xt_hi"], g * KC + k + 1)
                        nc.vector.tensor_tensor(xT_lo[:, k, :], (bank_q, bank_k)[k][:, :], xT_hi[:, k, :].bitcast(F32),
                                                ALU.subtract).then_inc(s["xt_lo"], 1)
                    dve.wait_ge(s["ct_hi"], g + 1)
                    nc.vector.tensor_tensor(cT_lo[:, :, :].rearrange("p k n -> p (k n)"), bank_m[:, 0:KC * GB * SK],
                                            cT_hi[:, :, :].bitcast(F32).rearrange("p k n -> p (k n)"),
                                            ALU.subtract).then_inc(s["ct_lo"], 1)

                def values_lo(g):
                    for j in range(2 * GB):
                        dve.wait_ge(s["v_hi_s"], g * 2 * GB + j + 1)
                        b, h = j // 2, j % 2
                        vin = v_banks[j][0:SK, :].rearrange("p (a e d) -> p a e d", e=2, d=D)
                        sel = lambda v: v[:, b, h * PAIRS // 2:(h + 1) * PAIRS // 2, :] \
                            .rearrange("p a (e d) -> p a e d", d=D)[:, :, 0:3:2, :]
                        nc.vector.tensor_tensor(sel(v_lo), vin, sel(v_hi).bitcast(F32), ALU.subtract).then_inc(s["v_lo_s"], 1)

                def qk_lo(n, p):
                    dve.wait_ge(s["q_hi_s"], n + 1)
                    nc.vector.scalar_tensor_tensor(out=q_lo[:, :], in0=bank_q[:, :], scalar=bqk[:, 0, p:p + 1],
                                                   in1=q_hi[:, :].bitcast(F32), op0=ALU.add, op1=ALU.subtract).then_inc(s["q_lo_s"], 1)
                    dve.wait_ge(s["k_hi_s"], 2 * (n + 1))
                    for e in range(2):
                        r = slice(e * D, (e + 1) * D)
                        nc.vector.scalar_tensor_tensor(
                            out=k_lo[r, :, e * SK:(e + 1) * SK],
                            in0=bank_k[r, 0:GB * SK].rearrange("p (b k) -> p b k", b=GB), scalar=bqk[r, 1, p:p + 1],
                            in1=k_hi[r, :, e * SK:(e + 1) * SK].bitcast(F32), op0=ALU.add, op1=ALU.subtract).then_inc(s["k_lo_s"], 1)

                def maxima(n, p):
                    for b in range(GB):
                        dve.wait_ge(s["sc"], 1 + n * GB + b + 1)
                        sc = bank_s[b][:, 0:QT * SK2].rearrange("p (t h k) -> p t h k", t=QT, h=2)
                        nc.vector.tensor_reduce(nmax[:, p % 2, b * QT:(b + 1) * QT, :], sc, AX.X, ALU.max,
                                                negate=True).then_inc(s["mx"], 1)

                def reciprocals(n, p, b):
                    dve.wait_ge(s["ex"], 1 + n * GB + b + 1)
                    nc.vector.reciprocal(rsum[:, p % 2, b * QT:(b + 1) * QT, :],
                                         ssum[:, p % 2, b * QT:(b + 1) * QT, :]).then_inc(s["rc"], 1)

                def pt_lo(n):
                    for b in range(GB):
                        dve.wait_ge(s["p_hi"], n * GB + b + 1)
                        nc.vector.tensor_tensor(pT_lo[:, b, :, :, :].rearrange("p h t q -> p (h t q)"), bank_t[b][0:SK, :],
                                                pT_hi[:, b, :, :, :].bitcast(F32).rearrange("p h t q -> p (h t q)"),
                                                ALU.subtract).then_inc(s["p_lo"], 1)

                def a_lo(n, p):
                    dve.wait_ge(s["a_hi"], n + 1)
                    nc.vector.scalar_tensor_tensor(out=aT_lo[:, p, :], in0=bank_o[:, :], scalar=bqk[:, 2, p:p + 1],
                                                   in1=aT_hi[:, p, :].bitcast(F32), op0=ALU.add, op1=ALU.subtract).then_inc(s["a_lo"], 1)

                dve.wait_ge(s["xg_in"], 16)
                x_tile = lambda t: xg[:, t, :]
                sums(x_tile, range(GT))
                statistics(0)
                dve.wait_ge(s["bo_in"], 16)
                nc.vector.tensor_tensor(xall[:, 2:GT, :], xg[:, 2:GT, :],
                                        bo_bc[:, :].rearrange("p (a c) -> p a c", a=1).broadcast_to([P, 2, C]),
                                        ALU.add).then_inc(s["xbo"], 1)
                dve.wait_ge(s["xbo"], 2)
                for tiles in LN_TILES:
                    normalize(x_tile, "ln1", 0, x_tile, tiles)
                weight_lo(0)
                dve.wait_ge(s["const"], 6)
                transposed(0)
                weight_lo(1)
                values_lo(0)
                dve.wait_ge(s["bias_in"], 48)
                nc.vector.tensor_scalar(bqk[:, 0, :], bqk[:, 0, :], SCALE, None, ALU.mult).then_inc(s["bq_s"], 1)
                weight_lo(2)
                dve.wait_ge(s["bq_s"], 1)
                qk_lo(0, 0)
                add_mask(0)

                def turn(g):
                    n = g * PAIRS
                    maxima(n, 0)
                    reciprocals(n, 0, 0)
                    qk_lo(n + 1, 1)
                    reciprocals(n, 0, 1)

                def body(g, more):
                    for p in range(1, PAIRS):
                        n = g * PAIRS + p
                        maxima(n, p)
                        reciprocals(n, p, 0)
                        pt_lo(n - 1)
                        if p + 1 < PAIRS:
                            qk_lo(n + 1, p + 1)
                        elif more:
                            transposed(g + 1)
                        reciprocals(n, p, 1)
                        a_lo(n - 1, p - 1)
                        if more and p == 1:
                            dve.wait_ge(s["xg_in"], 16 * (g + 2))
                            sums(x_tile, range(GT))
                            statistics(2 * g + 1)
                        if more and p >= PAIRS - 1 - len(LN_TILES) and p < PAIRS - 1:
                            dve.wait_ge(s["xbo"], 2 * (g + 2))
                            normalize(x_tile, "ln1", 2 * g + 1, x_tile, LN_TILES[p - (PAIRS - 1 - len(LN_TILES))])
                    n = (g + 1) * PAIRS
                    if more:
                        add_mask(g + 1)
                        qk_lo(n, 0)
                    pt_lo(n - 1)
                    if more:
                        turn(g + 1)
                    a_lo(n - 1, PAIRS - 1)
                    if more:
                        values_lo(g + 1)
                    x2_tile = lambda t: x2g[:, t, :]
                    for h in range(2):
                        dve.wait_ge(s["wo_d"], 1 + g * 2 + h + 1)
                        if h == 0:
                            dve.wait_ge(s["x2_kept"], 1 + 2 * g)
                            dve.wait_ge(s["xbo"], 2 * (g + 1))
                        xa = xall[:, bass.ds(g * GT + 2 * h, 2), :]
                        nc.vector.tensor_tensor(x2g[:, 2 * h:2 * h + 2, :], (bank_m, bank_o)[h][:, :].rearrange("p (t c) -> p t c", t=2), xa,
                                                ALU.add).then_inc(s["x2"], 1)
                        dve.wait_ge(s["x2"], 1 + g * 2 + h + 1)
                        sums(x2_tile, range(2 * h, 2 * h + 2))
                    stat = 2 * g + (2 if more else 1)
                    statistics(stat)
                    normalize(x2_tile, "ln2", stat,
                              lambda t: xrows[:, bass.ds(g * GT + t, 1), 0:C].rearrange("p a c -> p (a c)"))
                turn(0)
                with dve.Fori(0, G - 1) as g:
                    body(g, True)
                body(G - 1, False)

            @block.tensor
            def _(pe):
                count_from_one(pe, "sc pv wo_d tp")

                def transposed(g):
                    pe.wait_ge(s["ln1"], (g + 1) * len(LN_TILES))
                    pe.wait_ge(s["q_lo_s"], 1 + g * PAIRS)
                    pe.wait_ge(s["k_lo_s"], 1 + 2 * g * PAIRS)
                    for k in range(KC):
                        for t in range(GT):
                            last = nc.tensor.transpose((bank_q, bank_k)[k][:, t * P:(t + 1) * P], xg[:, t, k * P:(k + 1) * P], ident[:, :])
                        last.then_inc(s["xt"], 1)
                    pe.wait_ge(s["ctx_in"], 16 * (g + 1))
                    for k in range(KC):
                        for b in range(GB):
                            o = (k * GB + b) * SK
                            last = nc.tensor.transpose(bank_m[:, o:o + SK], ctxb[:, b, k * P:(k + 1) * P], ident[0:SK, 0:SK])
                    last.then_inc(s["ct"], 1)

                def project_values(g):
                    pe.wait_ge(s["ct_lo"], g + 1)
                    pe.wait_ge(s["w_lo"], 1)
                    for j in range(2 * GB):
                        b, h = j // 2, j % 2
                        if j < 2:
                            pe.wait_ge(s["p_lo"], 1 + g * PAIRS * GB)
                        if j == 3:
                            pe.wait_ge(s["a_lo"], 1 + g * PAIRS)
                        for k in range(KC):
                            last = three(pe, v_banks[j][0:SK, :],
                                         lambda lo: (cT_lo if lo else cT_hi)[:, k, b * SK:(b + 1) * SK],
                                         lambda lo: w_of(0, lo)[:, k, h * 512:(h + 1) * 512], k == 0, k == KC - 1)
                        last.then_inc(s["vp"], 1)

                def qk(n, p, ct):
                    pe.wait_ge(s["q_lo_s"], 1 + n)
                    pe.wait_ge(s["xt_lo"], ct * KC)
                    pe.wait_ge(s["ct_lo"], ct)
                    pe.wait_ge(s["w_lo"], 3)
                    for k in range(KC):
                        last = three(pe, bank_q[:, :], lambda lo: w_of(2, lo)[:, k, p * P:(p + 1) * P],
                                     lambda lo: (xT_lo if lo else xT_hi)[:, k, :], k == 0, k == KC - 1)
                    last.then_inc(s["qk_q"], 1)
                    pe.wait_ge(s["k_lo_s"], 1 + 2 * n)
                    for k in range(KC):
                        last = three(pe, bank_k[:, 0:GB * SK], lambda lo: w_of(1, lo)[:, k, p * P:(p + 1) * P],
                                     lambda lo: (cT_lo if lo else cT_hi)[:, k, :], k == 0, k == KC - 1)
                    last.then_inc(s["qk_k"], 1)

                def scores(g, n, p):
                    pe.wait_ge(s["q_lo_s"], 1 + n + 1)
                    pe.wait_ge(s["k_lo_s"], 1 + 2 * (n + 1))
                    if p == 0:
                        pe.wait_ge(s["mb"], g + 1)
                    for b in range(GB):
                        pe.wait_ge(s["ex"], 1 + ((n - 1) * GB + b + 1 if p else n * GB))
                        for t in range(QT):
                            o = bank_s[b][:, t * SK2:(t + 1) * SK2]
                            q = slice((b * QT + t) * P, (b * QT + t + 1) * P)
                            three(pe, o, lambda lo: (q_lo if lo else q_hi)[:, q],
                                  lambda lo: (k_lo if lo else k_hi)[:, b, :], True, False)
                            last = nc.tensor.matmul(o, identb[:, :], maskb[:, b * QT + t, :, :], start=False, stop=True)
                        last.then_inc(s["sc"], 1)

                def transposes(g, n, p):
                    for b in range(GB):
                        pe.wait_ge(s["nrm"], n * GB + b + 1)
                        if p:
                            pe.wait_ge(s["p_lo"], 1 + (n - 1) * GB + b + 1)
                        else:
                            pe.wait_ge(s["v_lo_s"], g * 2 * GB + 2)
                        for h in range(2):
                            for t in range(QT):
                                o = (h * QT + t) * P
                                last = nc.tensor.transpose(bank_t[b][0:SK, o:o + P], pr[:, p % 2, b * QT + t, h, :], ident[:, :])
                        last.then_inc(s["tp"], 1)

                def attend(g, n, p):
                    pe.wait_ge(s["a_lo"], 1 + n)
                    if p == 0:
                        pe.wait_ge(s["v_lo_s"], (g + 1) * 2 * GB)
                        pe.wait_ge(s["x2"], 1 + g * 2)
                    for b in range(GB):
                        pe.wait_ge(s["p_lo"], 1 + n * GB + b + 1)
                        o = bank_o[:, b * S:(b + 1) * S]
                        for h in range(2):
                            last = three(pe, o, lambda lo: (v_lo if lo else v_hi)[:, b, p, h * D:h * D + P],
                                         lambda lo: (pT_lo if lo else pT_hi)[:, b, h, :, :], h == 0, h == 1)
                    last.then_inc(s["pv"], 1)

                pe.wait_ge(s["const"], 2)
                transposed(0)
                project_values(0)
                qk(0, 0, 1)
                scores(0, 0, 0)
                qk(1, 1, 1)

                def body(g, more):
                    for p in range(1, PAIRS):
                        n = g * PAIRS + p
                        scores(g, n, p)
                        transposes(g, n - 1, p - 1)
                        if p + 1 < PAIRS:
                            qk(n + 1, p + 1, g + 1)
                        elif more:
                            transposed(g + 1)
                        attend(g, n - 1, p - 1)
                    n = (g + 1) * PAIRS
                    if more:
                        qk(n, 0, g + 2)
                    transposes(g, n - 1, PAIRS - 1)
                    if more:
                        scores(g + 1, n, 0)
                        qk(n + 1, 1, g + 2)
                    attend(g, n - 1, PAIRS - 1)
                    if more:
                        project_values(g + 1)
                        pe.wait_ge(s["v_lo_s"], (g + 2) * 2 * GB)
                    pe.wait_ge(s["a_lo"], 1 + n)
                    pe.wait_ge(s["wo_lo"], 1)
                    for h in range(2):
                        for t in range(2):
                            for p in range(PAIRS):
                                q = slice((2 * h + t) * P, (2 * h + t + 1) * P)
                                last = three(pe, (bank_m, bank_o)[h][:, t * C:(t + 1) * C], lambda lo: (aT_lo if lo else aT_hi)[:, p, q],
                                             lambda lo: w_of(3, lo)[:, p, :], p == 0, p == PAIRS - 1)
                        last.then_inc(s["wo_d"], 1)
                with pe.Fori(0, G - 1) as g:
                    body(g, True)
                body(G - 1, False)

        NF = F // P
        TE = TILES * NE
        out_f = out.rearrange("b s c -> (b s) c")
        out_v = out.rearrange("b (t p) c -> p (b t) c", p=P)
        qo.close()
        we1 = sb("we1", [P, 2, KC, F], F32)
        we2 = sb("we2", [P, 2, NF, C], F32)
        r = ExitStack()
        zT_hi = sb("zT_hi", [P, KC, TILES * P], F32R, r)
        zT_lo = sb("zT_lo", [P, KC, TILES * P], F32R, r)
        sh = sb("sh", [P, 2, GW], F32, r)
        hT_hi = sb("hT_hi", [P, NF, GW], F32R, r)
        hT_lo = sb("hT_lo", [P, NF, GW], F32R, r)
        wg_raw = sb("wg_raw", [P, KC, NE], F32, r)
        wg_hi = sb("wg_hi", [P, KC, NE], F32R, r)
        wg_lo = sb("wg_lo", [P, KC, NE], F32R, r)
        bs1c = sb("bs1c", [P, NF], F32, r)
        bs2_bc = sb("bs2_bc", [P, C], F32, r)
        rt = {n: sb("rt_" + n, [P, TILES, NE], F32, r) for n in ("d", "p", "eq", "oh1", "oh2", "p2", "tmp")}
        rm = {n: sb("rm_" + n, [P, TILES], F32, r) for n in ("m", "sum", "rs", "m1", "t1", "m2", "t2", "den", "rden", "w1", "w2", "p1", "p2")}
        assign = sb("assign", [P, NE, TILES], BF16, r)
        inc = sb("inc", [P, NE, TILES], F32, r)
        pos = sb("pos", [P, NE, TILES], F32, r)
        reset = sb("reset", [P, NE, TILES], F32, r)
        below = sb("below", [P, P], BF16, r)
        onesb = sb("onesb", [P, P], BF16, r)
        iotas = sb("iotas", [P, NE + TILES + NBLK], I32, r)
        falling = sb("falling", [P, NE], F32, r)
        blockno = sb("blockno", [P, NBLK], F32, r)
        cnt = sb("cnt", [P, NE], F32, r)
        cnti = sb("cnti", [P, NE], I32, r)
        blocks = sb("blocks", [P, NE], F32, r)
        ones8 = sb("ones8", [P, NE], F32, r)
        ends = sb("ends", [P, NE], F32, r)
        starts = sb("starts", [P, NE], F32, r)
        cmpb = sb("cmpb", [P, NBLK, NE - 1], F32, r)
        ebf = sb("ebf", [P, NBLK], F32, r)
        place = sb("place", [P, 2, TILES], I32, r)
        r.close()

        s.update({n: sem(n) for n in """zt_in ztp z_hi z_lo wgin wsh_hi wsh_lo lgt rexp rdve rpre rios
                  wsin bsin xb2 hp silu h_hi h_lo yp ysum outst scat iot rowsready placed routed""".split()})
        ws_in = [sem(f"ws_in{i}") for i in range(2)]
        ws_views = [ws1.rearrange("(k p) n -> p k n", p=P), ws2.rearrange("(k p) n -> p k n", p=P)]
        at_assign = []
        b1_bc, b2_bc = stage[:, 0, :].rearrange("p (s n) -> p s n", s=2), stage[:, 1, :].rearrange("p (e n) -> p e n", e=NE)
        s.update({n: sem(n) for n in ("b2in", "we_in")})

        def load_expert(sp, e):
            sp.dma_start(we1[:, e % 2, :, :], w1[e].rearrange("(k p) n -> p k n", p=P)).then_inc(s["we_in"], 16)
            sp.dma_start(we2[:, e % 2, :, :], w2[e].rearrange("(k p) n -> p k n", p=P)).then_inc(s["we_in"], 16)

        def load_b1(sp, e):
            sp.dma_start(b1_bc[:, e % 2, :], b1[e:e + 1, :].broadcast_to([P, F])).then_inc(s["we_in"], 16)
        zbanks = [bank_q, bank_k, bank_m, bank_o]

        with nc.Block() as block:
            @block.sync
            def _(sp):
                for i in range(2):
                    k = ws_views[i].shape[1]
                    sp.dma_start(stage[:, i, :].rearrange("p (k n) -> p k n", k=k), ws_views[i]).then_inc(ws_in[i], 16)
                for e in range(2):
                    load_expert(sp, e)
                sp.wait_ge(s["wsh_lo"], 2)
                for e in range(2):
                    load_b1(sp, e)
                sp.dma_start(b2_bc[:, :, :], b2.rearrange("(a e) c -> a e c", a=1).broadcast_to([P, NE, C])).then_inc(s["b2in"], 16)
                sp.wait_ge(s["we_in"], 48 * 2)
                sp.wait_ge(s["b2in"], 16)
                with sp.Fori(0, G) as g:
                    sp.wait_ge(s["ysum"], 1 + 2 * g + 2)
                    sp.dma_start(out_v[:, bass.ds(g * GT, GT), :], xall[:, bass.ds(g * GT, GT), :]).then_inc(s["outst"], 16)
                sp.wait_ge(s["outst"], 16 * G)

            @block.gpsimd
            def _(pool):
                nc.gpsimd.iota(iotas[:, 0:NE], pattern=[[-1, NE]], base=NE, channel_multiplier=0).then_inc(s["iot"], 1)
                nc.gpsimd.iota(iotas[:, NE:NE + TILES], pattern=[[P, TILES]], base=0, channel_multiplier=1).then_inc(s["iot"], 1)
                nc.gpsimd.iota(iotas[:, NE + TILES:], pattern=[[1, NBLK]], base=0, channel_multiplier=0).then_inc(s["iot"], 1)
                nc.gpsimd.memset(onesb[:, :], 1.0).then_inc(s["iot"], 1)
                nc.gpsimd.memset(ones8[:, :], 1.0).then_inc(s["iot"], 1)
                nc.gpsimd.memset(reset[:, :, :], 1.0).then_inc(s["iot"], 1)
                pool.wait_ge(s["iot"], 6)
                nc.gpsimd.affine_select(out=below[:, :], in_=onesb[:, :], compare_op=ALU.is_gt, fill=0.0, base=0,
                                        pattern=[[1, P]], channel_multiplier=-1).then_inc(s["iot"], 1)
                nc.gpsimd.memset(reset[:, :, 0:1], 0.0).then_inc(s["iot"], 1)
                for i in range(2):
                    pool.wait_ge(s["wsh_hi"], i + 1)
                    nc.gpsimd.tensor_tensor(wt_lo[i], stage[:, i, :], wt_hi[i].bitcast(F32),
                                            ALU.subtract).then_inc(s["wsh_lo"], 1)
                for f in range(NF):
                    pool.wait_ge(s["h_hi"], f + 1)
                    nc.gpsimd.tensor_tensor(hT_lo[:, f, :], sh[:, f % 2, :], hT_hi[:, f, :].bitcast(F32), ALU.subtract).then_inc(s["h_lo"], 1)
                pool.wait_ge(s["placed"], 1)
                for t in range(TILES):
                    for c in range(2):
                        nc.gpsimd.indirect_dma_start(
                            out=slots, out_offset=bass.IndirectOffsetOnAxis(ap=place[:, c, t:t + 1].bitcast(U32), axis=0),
                            in_=xrows[:, t, :], in_offset=None).then_inc(s["scat"], 16)
                pool.wait_ge(s["scat"], 2 * TILES * 16)

            @block.scalar
            def _(act):
                count_from_one(act, "silu")
                act.dma_start(wg_raw[:, :, :], wg.rearrange("(k p) n -> p k n", p=P)).then_inc(s["wgin"], 16)
                act.dma_start(bs1c[:, :], bs1.rearrange("(a p) -> p a", p=P), allow_slow_non_contiguous=True).then_inc(s["bsin"], 16)
                act.dma_start(bs2_bc[:, :], bs2.rearrange("(a n) -> a n", a=1).broadcast_to([P, C])).then_inc(s["bsin"], 16)
                act.wait_ge(s["wgin"], 16)
                nc.scalar.activation(wg_hi[:, :, :], wg_raw[:, :, :], ACT.Copy).then_inc(s["wgin"], 1)
                for j in range(G * KC):
                    act.wait_ge(s["ztp"], j + 1)
                    nc.scalar.activation(zT_hi[:, j % KC, (j // KC) * GW:(j // KC + 1) * GW], zbanks[j % 4][:, :], ACT.Copy).then_inc(s["z_hi"], 1)
                for i in range(2):
                    act.wait_ge(ws_in[i], 16)
                    nc.scalar.activation(wt_hi[i], stage[:, i, :], ACT.Copy).then_inc(s["wsh_hi"], 1)
                act.wait_ge(s["rdve"], 2)
                nc.scalar.activation(rt["p"][:, :, :], rt["d"][:, :, :], ACT.Exp).then_inc(s["rexp"], 1)
                act.wait_ge(s["bsin"], 32)
                def shared(g):
                    for f in range(NF):
                        n = g * NF + f
                        act.wait_ge(s["hp"], n + 1)
                        act.wait_ge(s["h_lo"], 1 + (n - 1 if f else g * NF))
                        nc.scalar.activation(sh[:, f % 2, :], bank_s[f % 2][:, :], ACT.Silu, bias=bs1c[:, f:f + 1]).then_inc(s["silu"], 1)
                        act.wait_ge(s["silu"], 1 + n + 1)
                        if f == 0:
                            act.wait_ge(s["yp"], 1 + 2 * g)
                        nc.scalar.activation(hT_hi[:, f, :], sh[:, f % 2, :], ACT.Copy).then_inc(s["h_hi"], 1)
                shared(0)
                with act.Fori(1, G) as g:
                    shared(g)

            @block.vector
            def _(dve):
                count_from_one(dve, "h_lo ysum")
                steps = [0]

                def link(ins):
                    steps[0] += 1
                    ins.then_inc(s["rdve"], 1)
                    dve.wait_ge(s["rdve"], steps[0])

                def over(v, n):
                    return v.rearrange("p (t a) -> p t a", a=1).broadcast_to([P, v.shape[1], n])

                dve.wait_ge(s["wgin"], 17)
                nc.vector.tensor_tensor(wg_lo[:, :, :], wg_raw[:, :, :], wg_hi[:, :, :].bitcast(F32), ALU.subtract).then_inc(s["wgin"], 1)
                for j in range(G * KC):
                    dve.wait_ge(s["z_hi"], j + 1)
                    c = slice((j // KC) * GW, (j // KC + 1) * GW)
                    nc.vector.tensor_tensor(zT_lo[:, j % KC, c], zbanks[j % 4][:, :], zT_hi[:, j % KC, c].bitcast(F32), ALU.subtract).then_inc(s["z_lo"], 1)
                lg = bank_t[0][:, 0:TE].rearrange("p (t e) -> p t e", e=NE)
                dve.wait_ge(s["lgt"], 1)
                link(nc.vector.tensor_reduce(rm["m"][:, :], lg, AX.X, ALU.max))
                link(nc.vector.tensor_tensor(rt["d"][:, :, :], lg, over(rm["m"][:, :], NE), ALU.subtract))
                dve.wait_ge(s["rexp"], 1)
                link(nc.vector.tensor_reduce(rm["sum"][:, :], rt["p"][:, :, :], AX.X, ALU.add))
                link(nc.vector.reciprocal(rm["rs"][:, :], rm["sum"][:, :]))
                link(nc.vector.tensor_tensor(rt["p"][:, :, :], rt["p"][:, :, :], over(rm["rs"][:, :], NE), ALU.mult))
                dve.wait_ge(s["iot"], 8)
                link(nc.vector.tensor_copy(falling[:, :], iotas[:, 0:NE]))
                link(nc.vector.tensor_copy(xrows[:, :, C].bitcast(I32), iotas[:, NE:NE + TILES]))
                link(nc.vector.tensor_copy(blockno[:, :], iotas[:, NE + TILES:]))
                fall = falling[:, :].rearrange("p (a e) -> p a e", a=1).broadcast_to([P, TILES, NE])

                def pick(prob, m, t, oh):
                    link(nc.vector.tensor_reduce(m, prob, AX.X, ALU.max))
                    link(nc.vector.tensor_tensor(rt["eq"][:, :, :], prob, over(m, NE), ALU.is_equal))
                    link(nc.vector.tensor_tensor(rt["eq"][:, :, :], rt["eq"][:, :, :], fall, ALU.mult))
                    link(nc.vector.tensor_reduce(t, rt["eq"][:, :, :], AX.X, ALU.max))
                    link(nc.vector.tensor_tensor(oh, fall, over(t, NE), ALU.is_equal))
                pick(rt["p"][:, :, :], rm["m1"][:, :], rm["t1"][:, :], rt["oh1"][:, :, :])
                link(nc.vector.scalar_tensor_tensor(out=rt["p2"][:, :, :], in0=rt["oh1"][:, :, :], scalar=-2.0,
                                                    in1=rt["p"][:, :, :], op0=ALU.mult, op1=ALU.add))
                pick(rt["p2"][:, :, :], rm["m2"][:, :], rm["t2"][:, :], rt["oh2"][:, :, :])
                link(nc.vector.tensor_tensor(assign[:, :, :].rearrange("p e t -> p t e"), rt["oh1"][:, :, :], rt["oh2"][:, :, :], ALU.add))
                at_assign.append(steps[0])
                link(nc.vector.scalar_tensor_tensor(out=rm["den"][:, :], in0=rm["m1"][:, :], scalar=1e-9,
                                                    in1=rm["m2"][:, :], op0=ALU.add, op1=ALU.add))
                link(nc.vector.reciprocal(rm["rden"][:, :], rm["den"][:, :]))
                link(nc.vector.tensor_tensor(rm["w1"][:, :], rm["m1"][:, :], rm["rden"][:, :], ALU.mult))
                link(nc.vector.tensor_tensor(rm["w2"][:, :], rm["m2"][:, :], rm["rden"][:, :], ALU.mult))
                link(nc.vector.tensor_tensor(rt["eq"][:, :, :], rt["oh1"][:, :, :], over(rm["w1"][:, :], NE), ALU.mult))
                link(nc.vector.tensor_tensor(rt["tmp"][:, :, :], rt["oh2"][:, :, :], over(rm["w2"][:, :], NE), ALU.mult))
                link(nc.vector.tensor_tensor(xrows[:, :, C + 1:C + 1 + NE], rt["eq"][:, :, :], rt["tmp"][:, :, :], ALU.add))
                dve.wait_ge(s["rpre"], 1)
                pre = bank_t[1][:, 0:TE].rearrange("p (e t) -> p e t", t=TILES)
                tot = bank_t[1][:, TE:2 * TE].rearrange("p (e t) -> p e t", t=TILES)
                flat1 = lambda v: v.rearrange("p e t -> p (e t)")
                link(nc.vector.tensor_tensor_scan(flat1(inc[:, :, :]), flat1(reset[:, :, :]), bank_t[1][:, TE:2 * TE], 0.0, ALU.mult, ALU.add))
                link(nc.vector.tensor_scalar(cnti[:, :], inc[:, :, TILES - 1], float(P - 1), None, ALU.add))
                link(nc.vector.tensor_scalar(cnti[:, :], cnti[:, :], 7, None, ALU.arith_shift_right))
                link(nc.vector.tensor_copy(blocks[:, :], cnti[:, :]))
                link(nc.vector.tensor_tensor_scan(ends[:, :], ones8[:, :], blocks[:, :], 0.0, ALU.mult, ALU.add))
                link(nc.vector.tensor_tensor(starts[:, :], ends[:, :], blocks[:, :], ALU.subtract))
                link(nc.vector.tensor_tensor(pos[:, :, :], inc[:, :, :], tot, ALU.subtract))
                link(nc.vector.tensor_tensor(pos[:, :, :], pos[:, :, :], pre, ALU.add))
                link(nc.vector.scalar_tensor_tensor(out=pos[:, :, :], in0=over(starts[:, :], TILES), scalar=float(P),
                                                    in1=pos[:, :, :], op0=ALU.mult, op1=ALU.add))
                for c in range(2):
                    link(nc.vector.tensor_tensor(rt["tmp"][:, :, :], rt[("oh1", "oh2")[c]][:, :, :],
                                                 pos[:, :, :].rearrange("p e t -> p t e"), ALU.mult))
                    link(nc.vector.tensor_reduce(rm[("p1", "p2")[c]][:, :], rt["tmp"][:, :, :], AX.X, ALU.add))
                    link(nc.vector.tensor_copy(place[:, c, :], rm[("p1", "p2")[c]][:, :]))
                nc.vector.tensor_copy(startsi[:, :], starts[:, :]).then_inc(s["placed"], 1)
                link(nc.vector.tensor_tensor(cmpb[:, :, :], over(blockno[:, :], NE - 1),
                                             starts[:, 1:NE].rearrange("p (a e) -> p a e", a=1).broadcast_to([P, NBLK, NE - 1]), ALU.is_ge))
                link(nc.vector.tensor_reduce(ebf[:, :], cmpb[:, :, :], AX.X, ALU.add))
                link(nc.vector.tensor_copy(ebi[:, 0, :], ebf[:, :]))
                link(nc.vector.tensor_scalar(ebi[:, 1, :], ebi[:, 0, :], 1, None, ALU.bitwise_and))
                dve.wait_ge(s["bsin"], 32)
                nc.vector.tensor_scalar(bs2_bc[:, :], bs2_bc[:, :], SHARED, None, ALU.mult).then_inc(s["xb2"], 1)
                dve.wait_ge(s["xb2"], 1)
                for g in range(G):
                    nc.vector.tensor_tensor(xall[:, g * GT:(g + 1) * GT, :], xall[:, g * GT:(g + 1) * GT, :],
                                            bs2_bc[:, :].rearrange("p (a c) -> p a c", a=1).broadcast_to([P, GT, C]),
                                            ALU.add).then_inc(s["xb2"], 1)
                dve.wait_ge(s["xb2"], 1 + G)
                def shared_sum(g):
                    for h in range(2):
                        dve.wait_ge(s["yp"], 1 + 2 * g + h + 1)
                        xa = xall[:, bass.ds(g * GT + 2 * h, 2), :].rearrange("p t c -> p (t c)")
                        nc.vector.scalar_tensor_tensor(out=xa, in0=(bank_m, bank_o)[h][:, :], scalar=SHARED, in1=xa,
                                                       op0=ALU.mult, op1=ALU.add).then_inc(s["ysum"], 1)
                shared_sum(0)
                with dve.Fori(1, G) as g:
                    for f in range(NF):
                        dve.wait_ge(s["h_hi"], g * NF + f + 1)
                        nc.vector.tensor_tensor(hT_lo[:, f, :], sh[:, f % 2, :], hT_hi[:, f, :].bitcast(F32), ALU.subtract).then_inc(s["h_lo"], 1)
                    shared_sum(g)

            @block.tensor
            def _(pe):
                count_from_one(pe, "yp")
                for j in range(G * KC):
                    k, c = j % KC, j // KC
                    if j >= 4:
                        pe.wait_ge(s["z_lo"], j - 3)
                    for t in range(GT):
                        last = nc.tensor.transpose(zbanks[j % 4][:, t * P:(t + 1) * P], xrows[:, c * GT + t, k * P:(k + 1) * P], ident[:, :])
                    last.then_inc(s["ztp"], 1)
                pe.wait_ge(s["z_lo"], G * KC)
                pe.wait_ge(s["wgin"], 18)
                for t in range(TILES):
                    for k in range(KC):
                        last = three(pe, bank_t[0][:, t * NE:(t + 1) * NE], lambda lo: (zT_lo if lo else zT_hi)[:, k, t * P:(t + 1) * P],
                                     lambda lo: (wg_lo if lo else wg_hi)[:, k, :], k == 0, k == KC - 1)
                last.then_inc(s["lgt"], 1)

                def prefix():
                    pe.wait_ge(s["iot"], 8)
                    pe.wait_ge(s["rdve"], at_assign[0])
                    a = assign[:, :, :].rearrange("p e t -> p (e t)")
                    nc.tensor.matmul(bank_t[1][:, 0:TE], below[:, :], a, start=True, stop=True)
                    nc.tensor.matmul(bank_t[1][:, TE:2 * TE], onesb[:, :], a, start=True, stop=True).then_inc(s["rpre"], 1)
                pe.wait_ge(s["wsh_lo"], 2)

                def shared(g):
                    for f in range(NF):
                        n = g * NF + f
                        pe.wait_ge(s["silu"], 1 + (n - 1 if f else g * NF))
                        for k in range(KC):
                            last = three(pe, bank_s[f % 2][:, :], lambda lo: w_of(0, lo, ws_views[0])[:, k, f * P:(f + 1) * P],
                                         lambda lo: (zT_lo if lo else zT_hi)[:, k, bass.ds(g * GW, GW)], k == 0, k == KC - 1)
                        last.then_inc(s["hp"], 1)
                    if isinstance(g, int):
                        prefix()
                    pe.wait_ge(s["h_lo"], 1 + (g + 1) * NF)
                    for h in range(2):
                        pe.wait_ge(s["ysum"], 1 + 2 * g)
                        for t in range(2):
                            for f in range(NF):
                                q = slice((2 * h + t) * P, (2 * h + t + 1) * P)
                                last = three(pe, (bank_m, bank_o)[h][:, t * C:(t + 1) * C], lambda lo: (hT_lo if lo else hT_hi)[:, f, q],
                                             lambda lo: w_of(1, lo, ws_views[1])[:, f, :], f == 0, f == NF - 1)
                        last.then_inc(s["yp"], 1)
                shared(0)
                with pe.Fori(1, G) as g:
                    shared(g)

        U = 4
        e_ = ExitStack()
        xs = sb("xs", [P, U, ROW], F32, e_)
        xsT = sb("xsT", [P, 2, KC, P], F32, e_)
        hb = sb("hb", [P, 2, F], F32, e_)
        hbT = sb("hbT", [P, NF, P], F32, e_)
        yb = sb("yb", [P, 2, C], F32, e_)
        nop = sb("nop", [P, 1], F32, e_)
        nop_to = sb("nop_to", [P, 1], F32, e_)
        yw = sb("yw", [P, 2, C], F32, e_)
        e_.close()
        s.update({n: sem(n) for n in "we_ready xsT_p xsT_c g1 hbias hsilu hT_p hTc_act hTc_dve g2 yadd yw_s added nopped".split()})
        xs_in = [sem(f"xs_in{i}") for i in range(U)]
        bank_h, bank_x, bank_y, bank_hT = bank_s, bank_q, bank_m, bank_t
        LOOP = (NBLK - 3) // U

        def steps(eng, step):
            with eng.Fori(0, LOOP) as j:
                for u in range(U):
                    step(U * j + u, u, U, j)
            for i in range(U * LOOP, NBLK):
                step(i, i % U, NBLK - 1 - i, i // U)

        with nc.Block() as block:
            @block.sync
            def _(sp):
                for e in range(2, NE):
                    sp.wait_ge(s["g2"], 1 + sp.value_load(startsi[0:1, e - 1:e], min_val=0, max_val=NBLK))
                    load_expert(sp, e)
                    load_b1(sp, e)
                    sp.wait_ge(s["we_in"], 48 * (e + 1))
                    sp.sem_inc(s["we_ready"], 1)

            @block.gpsimd
            def _(pool):
                nc.gpsimd.memset(nop[:, :], 0.0).then_inc(s["nopped"], 1)
                pool.wait_ge(s["nopped"], 1)
                pool.dma_start(nop_to[:, :], nop[:, :]).then_inc(s["added"], 16)
                last_token = pool.to_reg(B * S - 1)

                def step(i, u, left, turn):
                    pool.wait_ge(s["yw_s"], i + 1)
                    pool.wait_ge(s["added"], 16 * (i + 1))
                    pool.wait_ge(s["nopped"], i + 1)
                    nc.gpsimd.tensor_tensor(nop[:, :], nop[:, :], nop[:, :], ALU.add).then_inc(s["nopped"], 1)
                    nc.gpsimd.indirect_dma_start(
                        out=out_f, out_offset=bass.IndirectOffsetOnAxis(ap=xs[:, u, C:C + 1].bitcast(U32), axis=0),
                        in_=yw[:, u % 2, :], in_offset=None, bounds_check=last_token, oob_is_err=False,
                        compute_op=ALU.add).then_inc(s["added"], 16)
                steps(pool, step)
                pool.wait_ge(s["added"], 16 * (NBLK + 1))

            @block.scalar
            def _(act):
                count_from_one(act, "hTc_act")
                def load(i, u):
                    act.dma_start(xs[:, u, :], slots[bass.ds(i * P, P), :]).then_inc(xs_in[u], 16)

                def silu(i, u):
                    for h in range(2):
                        act.wait_ge(s["hbias"], 2 * i + h + 1)
                        hv = hb[:, u % 2, h * 512:(h + 1) * 512]
                        nc.scalar.activation(hv, hv, ACT.Silu).then_inc(s["hsilu"], 1)

                def rows_t(i, u):
                    act.wait_ge(s["xsT_p"], i + 1)
                    nc.scalar.activation(xsT[:, u % 2, :, :], bank_x[:, 0:KC * P], ACT.Copy).then_inc(s["xsT_c"], 1)

                def step(i, u, left, turn):
                    act.wait_ge(s["hT_p"], 2 * i + 1)
                    nc.scalar.activation(hbT[:, 0:NF // 2, :], bank_hT[0][:, :], ACT.Copy).then_inc(s["hTc_act"], 1)
                    if left >= 1:
                        silu(i + 1, u + 1)
                    if left >= 2:
                        rows_t(i + 2, u + 2)
                    if left >= 3:
                        act.wait_ge(s["added"], 16 * (i + 1))
                        load(i + 3, (u + 3) % U)
                for i in range(3):
                    load(i, i)
                rows_t(0, 0)
                silu(0, 0)
                rows_t(1, 1)
                steps(act, step)

            @block.vector
            def _(dve):
                count_from_one(dve, "hTc_dve yadd")
                def bias(i, u):
                    slot = dve.value_load(ebi[0:1, 1, bass.ds(i, 1)], min_val=0, max_val=1)
                    for h in range(2):
                        dve.wait_ge(s["g1"], 2 * i + h + 1)
                        nc.vector.tensor_tensor(hb[:, u % 2, h * 512:(h + 1) * 512], bank_h[h][:, :],
                                                b1_bc[:, bass.ds(slot, 1), h * 512:(h + 1) * 512].rearrange("p a n -> p (a n)"),
                                                ALU.add).then_inc(s["hbias"], 1)

                def step(i, u, left, turn):
                    dve.wait_ge(s["hT_p"], 2 * i + 2)
                    nc.vector.tensor_copy(hbT[:, NF // 2:, :].rearrange("p f q -> p (f q)"), bank_hT[1][:, :]).then_inc(s["hTc_dve"], 1)
                    if left >= 1:
                        bias(i + 1, u + 1)
                    e = dve.value_load(ebi[0:1, 0, bass.ds(i, 1)], min_val=0, max_val=NE - 1)
                    dve.wait_ge(s["g2"], 1 + i + 1)
                    nc.vector.tensor_tensor(yb[:, u % 2, :], bank_y[:, 0:C], b2_bc[:, bass.ds(e, 1), :].rearrange("p a c -> p (a c)"),
                                            ALU.add).then_inc(s["yadd"], 1)
                    dve.wait_ge(s["added"], 16 * (i + 1))
                    dve.wait_ge(s["yadd"], 1 + i + 1)
                    nc.vector.tensor_scalar(yw[:, u % 2, :], yb[:, u % 2, :], xs[:, u, bass.ds(e + (C + 1), 1)], None,
                                            ALU.mult).then_inc(s["yw_s"], 1)
                bias(0, 0)
                steps(dve, step)

            @block.tensor
            def _(pe):
                count_from_one(pe, "g2")
                pe.sem_inc(s["we_ready"], 2)
                def rows_t(i, u, at):
                    pe.wait_ge(xs_in[u], 16 * (at + 1))
                    pe.wait_ge(s["xsT_c"], i)
                    for k in range(KC):
                        last = nc.tensor.transpose(bank_x[:, k * P:(k + 1) * P], xs[:, u, k * P:(k + 1) * P], ident[:, :])
                    last.then_inc(s["xsT_p"], 1)

                def up(i, u):
                    e = pe.value_load(ebi[0:1, 0, bass.ds(i, 1)], min_val=0, max_val=NE - 1)
                    slot = pe.value_load(ebi[0:1, 1, bass.ds(i, 1)], min_val=0, max_val=1)
                    pe.wait_ge(s["we_ready"], e + 1)
                    pe.wait_ge(s["xsT_c"], i + 1)
                    for h in range(2):
                        pe.wait_ge(s["hbias"], 2 * i)
                        for k in range(KC):
                            last = nc.tensor.matmul(bank_h[h][:, :], xsT[:, u % 2, k, :],
                                                    we1[:, bass.ds(slot, 1), k, h * 512:(h + 1) * 512].rearrange("p a n -> p (a n)"),
                                                    start=k == 0, stop=k == KC - 1)
                        last.then_inc(s["g1"], 1)

                def step(i, u, left, turn):
                    pe.wait_ge(s["hTc_act"], 1 + i)
                    pe.wait_ge(s["hTc_dve"], 1 + i)
                    for h in range(2):
                        pe.wait_ge(s["hsilu"], 2 * i + h + 1)
                        for f in range(NF // 2):
                            o = (h * NF // 2 + f) * P
                            last = nc.tensor.transpose(bank_hT[h][:, f * P:(f + 1) * P], hb[:, u % 2, o:o + P], ident[:, :])
                        last.then_inc(s["hT_p"], 1)
                    if left >= 1:
                        up(i + 1, u + 1)
                    if left >= 2:
                        rows_t(i + 2, (u + 2) % U, turn + (u + 2) // U)
                    slot = pe.value_load(ebi[0:1, 1, bass.ds(i, 1)], min_val=0, max_val=1)
                    pe.wait_ge(s["hTc_act"], 1 + i + 1)
                    pe.wait_ge(s["hTc_dve"], 1 + i + 1)
                    pe.wait_ge(s["yadd"], 1 + i)
                    for f in range(NF):
                        last = nc.tensor.matmul(bank_y[:, 0:C], hbT[:, f, :], we2[:, bass.ds(slot, 1), f, :].rearrange("p a c -> p (a c)"),
                                                start=f == 0, stop=f == NF - 1)
                    last.then_inc(s["g2"], 1)
                rows_t(0, 0, 0)
                up(0, 0)
                rows_t(1, 1, 0)
                steps(pe, step)


_INS = ['x', 'ctx_1024', 'mask_BxSxS2_bk1'] + ['L0_xattn_' + n for n in ('Wq', 'bq', 'Wk', 'bk', 'Wv', 'bv', 'Wo', 'bo')] \
    + ['L0_ffn_' + n for n in ('Wg', 'W1', 'b1', 'W2', 'b2', 'Ws1', 'bs1', 'Ws2', 'bs2')]


def kernel(**inputs):
    import numpy as _np
    import concourse.bacc as _bacc
    from concourse import mybir as _mybir
    from concourse.bass_utils import run_bass_kernel_spmd as _run

    nc = _bacc.Bacc("TRN2", target_bir_lowering=False, num_devices=1)
    arrays, args = {}, []
    for name in _INS:
        a = _np.ascontiguousarray(inputs[name])
        arrays[f"in_{name}"] = a
        args.append(nc.dram_tensor(f"in_{name}", a.shape, _mybir.dt.from_np(a.dtype), kind="ExternalInput").ap())
    shape = inputs['x'].shape
    out = nc.dram_tensor("out_dram", shape, _mybir.dt.float32, kind="ExternalOutput").ap()
    xattn_moe_kernel(nc, *args, out)
    r = _run(nc, [arrays], core_ids=[0])
    return r.results[0]["out_dram"]
```
